# Optimizing a Trainium2 kernel written in Bass

```python
import numpy as np
import jax
import jax.numpy as jnp

def _softmax(x, axis=-1):
    return jax.nn.softmax(x, axis=axis)

def _gelu(x):
    return jax.nn.gelu(x, approximate=True)

def _silu(x):
    return jax.nn.silu(x)

def _sigmoid(x):
    return jax.nn.sigmoid(x)

def _layernorm(x, axis=-1, eps=1e-05):
    m = jnp.mean(x, axis=axis, keepdims=True)
    v = jnp.var(x, axis=axis, keepdims=True)
    return (x - m) / jnp.sqrt(v + eps)

def _scatter_add(tgt, idx, src, axis=0):
    return tgt.at[idx].add(src)

def _segment_sum(src, seg, n):
    return jax.ops.segment_sum(src, seg, n)
kernel_name = 'mk_gnn_ffn_d1_gnn_r32_9ae4b2'

def setup_inputs(seed: int=0):
    np.random.seed(seed)
    _w = jnp.asarray

    def _rec_inputs():
        import jax
        import jax.numpy as jnp
        _gk = jax.random.key(seed)
        x = -0.0002117 + 1 * jax.random.normal(jax.random.fold_in(_gk, 1), (3125, 256), jnp.float32)
        src = jax.random.randint(jax.random.fold_in(_gk, 2), (50000,), 0, 3125, jnp.int32)
        dst = jax.random.randint(jax.random.fold_in(_gk, 3), (50000,), 0, 3125, jnp.int32)
        _o = jnp.argsort(dst, stable=True)
        src = src[_o]
        dst = dst[_o]
        return (x, src, dst)
    x, src, dst = _rec_inputs()

    def _L0_gnn_setup():
        import jax, jax.numpy as jnp
        import numpy as np
        N_NODES = 3125
        N_EDGES = 9375
        D_MODEL = 256
        N_HEADS = 8
        D_HEAD = D_MODEL // N_HEADS

        def _layernorm(x, w, b, eps=1e-05):
            mu = jnp.mean(x, axis=-1, keepdims=True)
            var = jnp.var(x, axis=-1, keepdims=True)
            return (x - mu) * jax.lax.rsqrt(var + eps) * w + b
        key = jax.random.key(seed)
        ks = jax.random.split(key, 16)
        d, h = (D_MODEL, D_MODEL)
        s = 1.0 / np.sqrt(d)
        inp = {'x': jax.random.normal(ks[0], (N_NODES, d), dtype=jnp.float32), 'edge_index': jax.random.randint(ks[1], (2, N_EDGES), 0, N_NODES, dtype=jnp.int64), 'Wq': jax.random.normal(ks[2], (d, d), dtype=jnp.float32) * s, 'Wk': jax.random.normal(ks[3], (d, d), dtype=jnp.float32) * s, 'Wv': jax.random.normal(ks[4], (d, d), dtype=jnp.float32) * s, 'O_w': jax.random.normal(ks[5], (d, d), dtype=jnp.float32) * s, 'O_b': jnp.zeros((d,), dtype=jnp.float32), 'ln1_w': jnp.ones((d,), dtype=jnp.float32), 'ln1_b': jnp.zeros((d,), dtype=jnp.float32), 'f1_w': jax.random.normal(ks[6], (d, 2 * d), dtype=jnp.float32) * s, 'f1_b': jnp.zeros((2 * d,), dtype=jnp.float32), 'f2_w': jax.random.normal(ks[7], (2 * d, d), dtype=jnp.float32) / np.sqrt(2 * d), 'f2_b': jnp.zeros((d,), dtype=jnp.float32), 'ln2_w': jnp.ones((d,), dtype=jnp.float32), 'ln2_b': jnp.zeros((d,), dtype=jnp.float32), 'gru_w_ih': jax.random.normal(ks[8], (d, 3 * h), dtype=jnp.float32) * s, 'gru_w_hh': jax.random.normal(ks[9], (h, 3 * h), dtype=jnp.float32) * s, 'gru_b_ih': jnp.zeros((3 * h,), dtype=jnp.float32), 'gru_b_hh': jnp.zeros((3 * h,), dtype=jnp.float32)}
        return inp
    _L0_gnn_all = _L0_gnn_setup()
    _L0_gnn_in = {k: v for k, v in _L0_gnn_all.items() if k in ('Wq', 'Wk', 'Wv', 'O_w', 'O_b', 'ln1_w', 'ln1_b', 'f1_w', 'f1_b', 'f2_w', 'f2_b', 'ln2_w', 'ln2_b', 'gru_w_ih', 'gru_w_hh', 'gru_b_ih', 'gru_b_hh')}
    del _L0_gnn_all

    def _L0_ffn_setup():
        import jax, jax.numpy as jnp
        import numpy as np
        D_MODEL = 256
        EXPERT_DIM = 512
        NUM_EXPERTS = 8
        TOP_K = 2
        SEQ_LEN = 64
        BATCH = 2
        key = jax.random.key(seed)
        ks = jax.random.split(key, 8)
        s = 0.02
        x = jax.random.normal(ks[0], (SEQ_LEN, BATCH, D_MODEL), dtype=jnp.float32)
        Wg = jax.random.normal(ks[1], (D_MODEL, NUM_EXPERTS), dtype=jnp.float32) * s
        bg = jax.random.normal(ks[2], (NUM_EXPERTS,), dtype=jnp.float32) * s
        bias = jnp.zeros((NUM_EXPERTS,), dtype=jnp.float32)
        W1 = jax.random.normal(ks[3], (NUM_EXPERTS, D_MODEL, EXPERT_DIM), dtype=jnp.float32) * s
        b1 = jax.random.normal(ks[4], (NUM_EXPERTS, EXPERT_DIM), dtype=jnp.float32) * s
        W2 = jax.random.normal(ks[5], (NUM_EXPERTS, EXPERT_DIM, D_MODEL), dtype=jnp.float32) * s
        b2 = jax.random.normal(ks[6], (NUM_EXPERTS, D_MODEL), dtype=jnp.float32) * s
        return {'x': x, 'Wg': Wg, 'bg': bg, 'bias': bias, 'W1': W1, 'b1': b1, 'W2': W2, 'b2': b2}
    _L0_ffn_all = _L0_ffn_setup()
    _L0_ffn_in = {k: v for k, v in _L0_ffn_all.items() if k in ('Wg', 'bg', 'bias', 'W1', 'b1', 'W2', 'b2')}
    del _L0_ffn_all
    return {'x': x, 'src': src, 'dst': dst, 'L0_gnn_Wq': _L0_gnn_in['Wq'], 'L0_gnn_Wk': _L0_gnn_in['Wk'], 'L0_gnn_Wv': _L0_gnn_in['Wv'], 'L0_gnn_O_w': _L0_gnn_in['O_w'], 'L0_gnn_O_b': _L0_gnn_in['O_b'], 'L0_gnn_ln1_w': _L0_gnn_in['ln1_w'], 'L0_gnn_ln1_b': _L0_gnn_in['ln1_b'], 'L0_gnn_f1_w': _L0_gnn_in['f1_w'], 'L0_gnn_f1_b': _L0_gnn_in['f1_b'], 'L0_gnn_f2_w': _L0_gnn_in['f2_w'], 'L0_gnn_f2_b': _L0_gnn_in['f2_b'], 'L0_gnn_ln2_w': _L0_gnn_in['ln2_w'], 'L0_gnn_ln2_b': _L0_gnn_in['ln2_b'], 'L0_gnn_gru_w_ih': _L0_gnn_in['gru_w_ih'], 'L0_gnn_gru_w_hh': _L0_gnn_in['gru_w_hh'], 'L0_gnn_gru_b_ih': _L0_gnn_in['gru_b_ih'], 'L0_gnn_gru_b_hh': _L0_gnn_in['gru_b_hh'], 'L0_ffn_Wg': _L0_ffn_in['Wg'], 'L0_ffn_bg': _L0_ffn_in['bg'], 'L0_ffn_bias': _L0_ffn_in['bias'], 'L0_ffn_W1': _L0_ffn_in['W1'], 'L0_ffn_b1': _L0_ffn_in['b1'], 'L0_ffn_W2': _L0_ffn_in['W2'], 'L0_ffn_b2': _L0_ffn_in['b2']}

def reference(x, src, dst, L0_gnn_Wq, L0_gnn_Wk, L0_gnn_Wv, L0_gnn_O_w, L0_gnn_O_b, L0_gnn_ln1_w, L0_gnn_ln1_b, L0_gnn_f1_w, L0_gnn_f1_b, L0_gnn_f2_w, L0_gnn_f2_b, L0_gnn_ln2_w, L0_gnn_ln2_b, L0_gnn_gru_w_ih, L0_gnn_gru_w_hh, L0_gnn_gru_b_ih, L0_gnn_gru_b_hh, L0_ffn_Wg, L0_ffn_bg, L0_ffn_bias, L0_ffn_W1, L0_ffn_b1, L0_ffn_W2, L0_ffn_b2):
    import jax
    import jax.numpy as jnp

    def _L0_gnn_ref(x, edge_index, Wq, Wk, Wv, O_w, O_b, ln1_w, ln1_b, f1_w, f1_b, f2_w, f2_b, ln2_w, ln2_b, gru_w_ih, gru_w_hh, gru_b_ih, gru_b_hh):
        import jax, jax.numpy as jnp
        import numpy as np
        N_NODES = 3125
        N_EDGES = 9375
        D_MODEL = 256
        N_HEADS = 8
        D_HEAD = D_MODEL // N_HEADS

        def _layernorm(x, w, b, eps=1e-05):
            mu = jnp.mean(x, axis=-1, keepdims=True)
            var = jnp.var(x, axis=-1, keepdims=True)
            return (x - mu) * jax.lax.rsqrt(var + eps) * w + b
        N = x.shape[0]
        H, D = (N_HEADS, D_HEAD)
        Q = (x @ Wq).reshape(N, H, D)
        K = (x @ Wk).reshape(N, H, D)
        V = (x @ Wv).reshape(N, H, D)
        score = jnp.einsum('nhd,ngd->nhg', Q, K) / np.sqrt(D)
        score = jax.nn.softmax(score, axis=-1)
        x1 = jnp.einsum('nhg,ngd->nhd', score, V).reshape(N, H * D)
        src, dst = (edge_index[0], edge_index[1])
        msg = x1[dst] * x1[src]
        attn_out = jax.ops.segment_sum(msg, dst, num_segments=N)
        h = attn_out @ O_w + O_b
        h = x + h
        h = _layernorm(h, ln1_w, ln1_b)
        ffn = jax.nn.relu(h @ f1_w + f1_b) @ f2_w + f2_b
        h = _layernorm(h + ffn, ln2_w, ln2_b)
        gi = h @ gru_w_ih + gru_b_ih
        gh = h @ gru_w_hh + gru_b_hh
        gi_r, gi_z, gi_n = jnp.split(gi, 3, axis=-1)
        gh_r, gh_z, gh_n = jnp.split(gh, 3, axis=-1)
        r = jax.nn.sigmoid(gi_r + gh_r)
        z = jax.nn.sigmoid(gi_z + gh_z)
        n = jnp.tanh(gi_n + r * gh_n)
        return (1.0 - z) * n + z * h

    def _L0_ffn_ref(x, Wg, bg, bias, W1, b1, W2, b2):
        import jax, jax.numpy as jnp
        import numpy as np
        D_MODEL = 256
        EXPERT_DIM = 512
        NUM_EXPERTS = 8
        TOP_K = 2
        SEQ_LEN = 64
        BATCH = 2
        x_flat = x.reshape(-1, D_MODEL)
        gate_logits = x_flat @ Wg + bg + bias
        topk_vals, topk_idx = jax.lax.top_k(gate_logits, TOP_K)
        topk_w = jax.nn.softmax(topk_vals, axis=-1)
        combine = (jax.nn.one_hot(topk_idx, NUM_EXPERTS, dtype=x.dtype) * topk_w[..., None]).sum(axis=1)
        h = jax.nn.relu(jnp.einsum('td,edh->teh', x_flat, W1) + b1)
        y = jnp.einsum('teh,ehd->ted', h, W2) + b2
        out = jnp.einsum('ted,te->td', y, combine)
        return out.reshape(x.shape)
    edge_index = jnp.stack([src, dst])
    x = x + _L0_gnn_ref(_layernorm(x, axis=-1), edge_index, L0_gnn_Wq, L0_gnn_Wk, L0_gnn_Wv, L0_gnn_O_w, L0_gnn_O_b, L0_gnn_ln1_w, L0_gnn_ln1_b, L0_gnn_f1_w, L0_gnn_f1_b, L0_gnn_f2_w, L0_gnn_f2_b, L0_gnn_ln2_w, L0_gnn_ln2_b, L0_gnn_gru_w_ih, L0_gnn_gru_w_hh, L0_gnn_gru_b_ih, L0_gnn_gru_b_hh)
    x = x + _L0_ffn_ref(_layernorm(x, axis=-1)[None], L0_ffn_Wg, L0_ffn_bg, L0_ffn_bias, L0_ffn_W1, L0_ffn_b1, L0_ffn_W2, L0_ffn_b2)[0]
    return x

_drawn_inputs = setup_inputs


def setup_inputs(seed=0):
    import zlib

    import numpy as np

    out = dict(_drawn_inputs(seed))
    spreads = {'L0_gnn_O_b': (0.0, 0.1),
     'L0_gnn_ln1_w': (1.0, 0.2),
     'L0_gnn_ln1_b': (0.0, 0.1),
     'L0_gnn_f1_b': (0.0, 0.1),
     'L0_gnn_f2_b': (0.0, 0.1),
     'L0_gnn_ln2_w': (1.0, 0.2),
     'L0_gnn_ln2_b': (0.0, 0.1),
     'L0_gnn_gru_b_ih': (0.0, 0.1),
     'L0_gnn_gru_b_hh': (0.0, 0.346),
     'L0_ffn_bias': (0.0, 0.1)}
    factors = {'L0_ffn_bg': 6.056, 'L0_ffn_b1': 8.0, 'L0_ffn_b2': 5.655}
    for name, (base, spread) in spreads.items():
        noise = np.random.default_rng([zlib.crc32(name.encode()), seed]).standard_normal(out[name].shape)
        drawn = base * np.exp(spread * noise) if base else spread * noise
        out[name] = jnp.asarray(drawn.astype(out[name].dtype))
    for name, factor in factors.items():
        out[name] = (out[name] * factor).astype(out[name].dtype)
    return out
```

```python
import concourse.bass as bass
from concourse import mybir
from contextlib import ExitStack


def gnn_moe_layer(nc, x, src, dst, Wq, Wk, Wv, O_w, O_b, ln1_w, ln1_b, f1_w, f1_b, f2_w, f2_b,
                  ln2_w, ln2_b, w_ih, w_hh, b_ih, b_hh, Wg, bg, gbias, W1, b1, W2, b2, out):
    f32, f16, i32, u32 = mybir.dt.float32, mybir.dt.float16, mybir.dt.int32, mybir.dt.uint32
    ALU, ACT, AX = mybir.AluOpType, mybir.ActivationFunctionType, mybir.AxisListType.X
    ds = bass.ds

    N, D = x.shape
    C = D // 128
    H, DH = 8, 32
    HG = 128 // DH
    G = H // HG
    QB = 448
    NB = -(-N // QB)
    NP = NB * QB
    T = 4
    NT = QB // T
    E = src.shape[0]
    EP = 125
    EC = E // EP
    EB = 20
    RB = 10
    NTT = NB * T
    CELLS = NP * NP
    SPLIT = 512
    F = f1_w.shape[1]
    FT = F // 128
    NE, FE = W1.shape[0], W1.shape[2]
    ET = FE // 128
    SCALE = float(DH) ** -0.5
    EPS = 1e-5
    LAST = N - (NB - 1) * QB
    LROWS = LAST - (T - 1) * NT

    counts = nc.dram_tensor("edge_counts", (CELLS + 128, 1), f32, kind="Internal").ap()
    att_rows = nc.dram_tensor("att_rows", (-(-N // QB), QB // T, T * D), f32, kind="Internal").ap()
    keys_row = nc.dram_tensor("edge_keys", (EC * EP,), f32, kind="Internal").ap()

    ctx = ExitStack()
    with ctx:
        def sb(name, shape, dt=f32):
            return ctx.enter_context(nc.sbuf_tensor(name, shape, dt))

        def sem(name):
            return ctx.enter_context(nc.semaphore(name))

        KQ = sb("KQ", [128, 2 * NTT * QB])
        x1 = sb("x1", [NT, NTT, D])
        VR = sb("VR", [128, 6400])
        x_in = KQ[0:NT, 0:NTT * D].rearrange("p (r t d) -> p r t d", r=NB, t=T)
        x_ln = VR[0:NT, 2 * T * D:4 * T * D].rearrange("p (r t d) -> p r t d", r=2, t=T)
        xnT = VR[:, 4 * T * D:4 * T * D + 2 * C * QB].rearrange("p (r c n) -> p r c n", r=2, c=C)
        WQKV = sb("WQKV", [128, C * 3 * D])
        wqkv = WQKV[:, :].rearrange("p (c w) -> p c w", c=C)
        RR = sb("RR", [128, 2 * RB * EP])
        rows = RR[0:EP, :].rearrange("p (r m e) -> p r m e", r=2, m=RB)
        HB = sb("HB", [128, 6400])
        qkv = HB[0:NT, 0:2 * 3 * D].rearrange("p (r w) -> p r w", r=2)
        prod = HB[0:NT, 3 * D * 2:3 * D * 2 + H * H * DH]
        scores = HB[0:NT, 3584:3584 + 64]
        probs = HB[0:NT, 3648:3648 + 2 * 64].rearrange("p (r w) -> p r w", r=2)
        hmax = HB[0:NT, 3776:3784]
        hsum = HB[0:NT, 3784:3792]
        hinv = HB[0:NT, 3792:3800]
        shifted_s = HB[0:NT, 3808:3808 + 128].rearrange("p (r w) -> p r w", r=2)

        zeros = sb("zeros", [NT, NP // 4])
        ident = sb("ident", [128, 128])
        mean_var = sb("mean_var", [NT, NB * T, 2])
        rstd = sb("rstd", [NT, NB * T])
        stats = sb("stats", [NT, T, 6])
        halfneg = sb("halfneg", [NT, T])
        ve = sb("ve", [NT, T])
        src_i = RR[0:EP, 0:EC].bitcast(i32)
        dst_i = RR[0:EP, EC:2 * EC].bitcast(i32)
        key = sb("key", [EP, EC])
        key_t = RR[0:EC // 4, 2 * EC:2 * EC + 4 * EP]
        first_w = sb("first_w", [EP, EP])
        eq = sb("eq", [EP, EP])
        tally = sb("tally", [EP, EC])
        spare = sb("spare", [EP, 1])
        fresh = sb("fresh", [EP, EB])
        shifted = sb("shifted", [EP, EB])
        target = sb("target", [EP, EC], i32)
        sc_idx = sb("sc_idx", [EP, EB], i32)
        sc_val = sb("sc_val", [EP, EB])

        pair = [ctx.enter_context(nc.psum_tensor(f"pair{i}", [128, 2, 512], f32)) for i in range(4)]
        bank = [pair[i // 2][:, i % 2, :] for i in range(8)]

        W1s = KQ[:, 0:NE * C * FE].rearrange("p (e c f) -> p e c f", e=NE, c=C)
        W2s = KQ[:, 8192:8192 + NE * ET * D].rearrange("p (e f d) -> p e f d", e=NE, f=ET)
        act0 = 16384
        attB = KQ[:, act0:act0 + C * QB].rearrange("p (c n) -> p c n", c=C)
        hT = KQ[:, act0 + 896:act0 + 1792].rearrange("p (c n) -> p c n", c=C)
        hid = [KQ[:, act0 + 1792:act0 + 3584].rearrange("p (f n) -> p f n", f=4),
               VR[:, 0:1792].rearrange("p (f n) -> p f n", f=4)]
        h = KQ[0:NT, act0 + 3584:act0 + 4608].rearrange("p (t d) -> p t d", t=T)
        x2 = KQ[0:NT, act0 + 4608:act0 + 5632].rearrange("p (t d) -> p t d", t=T)
        acc = KQ[0:NT, act0 + 5632:act0 + 6656].rearrange("p (t d) -> p t d", t=T)
        xd = VR[0:NT, 1792:2816].rearrange("p (t d) -> p t d", t=T)
        rT = VR[:, 2816:3712].rearrange("p (c n) -> p c n", c=C)
        zT = VR[:, 3712:4608].rearrange("p (c n) -> p c n", c=C)
        nT = VR[:, 4608:5504].rearrange("p (c n) -> p c n", c=C)
        uT = VR[:, 5504:6400].rearrange("p (c n) -> p c n", c=C)
        Ow = HB[:, 0:512].rearrange("p (c d) -> p c d", c=C)
        F1 = HB[:, 512:1536].rearrange("p (c d) -> p c d", c=C)
        F2 = HB[:, 1536:2560].rearrange("p (c d) -> p c d", c=FT)
        Wih = HB[:, 2560:4096].rearrange("p (c d) -> p c d", c=C)
        Whh = HB[:, 4096:5632].rearrange("p (c d) -> p c d", c=C)
        vecs = WQKV[0:NT, :].rearrange("p (v d) -> p v d", v=6)
        slab = [KQ[0:NT, i * NTT * QB:(i + 1) * NTT * QB].rearrange("p (k n) -> p k n", k=NTT) for i in range(2)]
        attb = [VR[0:NT, r * T * D:(r + 1) * T * D].rearrange("p (t d) -> p t d", t=T) for r in range(2)]
        f1b = sb("f1b", [128, FT])
        bih = sb("bih", [128, 6])
        bhh = sb("bhh", [128, 6])
        brz = sb("brz", [128, 4])
        b1s = sb("b1s", [128, NE, ET])
        b2s = sb("b2s", [NE, D])
        Wgs = sb("Wgs", [128, C, NE])
        gb = sb("gb", [NT, 2, NE])
        lg = sb("lg", [NT, T, NE])
        top = sb("top", [NT, T, 8])
        topi = sb("topi", [NT, T, 8], u32)
        topf = sb("topf", [NT, T, 2])
        gap = sb("gap", [NT, T])
        eg = sb("eg", [NT, T])
        w1 = sb("w1", [NT, T])
        w2 = sb("w2", [NT, T])
        oh = sb("oh", [NT, 2, T, NE])
        comb = sb("comb", [NT, T, NE])
        combT = sb("combT", [NE, QB])
        iota8 = sb("iota8", [NT, NE])
        dmv = sb("dmv", [NT, T, 2])
        drs = sb("drs", [NT, T])
        dve_ = sb("dve_", [NT, T])

        S = {}
        for name in ("w_in x_in0 x_in1 x_in2 x_in3 x_in4 x_in5 x_in6 e_in consts zeros_set zeroed key_done key_tr key_row key_out rows_in0 rows_in1 "
                     "rows_used targets sc_copied scattered st_done mv_done pool_ve rstd_done ln_done tr_done tr_act tr_dve "
                     "proj qkv_done h_chain sc_done ex_done prob_done x1_done "
                     "chain "
                     "att_out0 att_out1 slab_in0 slab_in1 agg aggm dw_in dw_prep moe_in "
                     "d_x d_ho d_mv d_ve d_rs d_h d_hT d_hTe d_f1 d_fT d_f2 d_g d_tr d_w d_n d_gT d_gn d_y d_lg "
                     "d_acc0 d_dd d_ex d_comb d_cT d_cTe d_b2 d_h1 d_he d_ye d_acc d_out d_small").split():
            S[name] = sem(name)

        block = ctx.enter_context(nc.Block())
        def blk(b):
            return slice(b * QB, (b + 1) * QB) if isinstance(b, int) else ds(b * QB, QB)

        @block.sync
        def _(sp):
            for b in range(NB):
                if b < NB - 1:
                    sp.dma_start(x_in[:, b, :, :], x[b * QB:(b + 1) * QB, :].rearrange("(t p) d -> p t d", p=NT)).then_inc(S[f"x_in{b}"], 16)
                else:
                    full = (T - 1) * NT
                    sp.wait_ge(S["zeros_set"], 2)
                    sp.dma_start(x_in[:, b, 0:T - 1, :], x[b * QB:b * QB + full, :].rearrange("(t p) d -> p t d", p=NT)).then_inc(S[f"x_in{b}"], 16)
                    sp.dma_start(x_in[0:LROWS, b, T - 1, :], x[b * QB + full:N, :]).then_inc(S[f"x_in{b}"], 16)
                if b == 0:
                    sp.dma_start(src_i, src.rearrange("(p c) -> p c", p=EP)).then_inc(S["e_in"], 16)
                    sp.dma_start(dst_i, dst.rearrange("(p c) -> p c", p=EP)).then_inc(S["e_in"], 16)
                    for w, a in enumerate((Wq, Wk, Wv)):
                        sp.dma_start(wqkv[:, :, w * D:(w + 1) * D], a.rearrange("(c p) d -> p c d", p=128)).then_inc(S["w_in"], 16)
            sp.wait_ge(S["key_row"], 1)
            sp.dma_start(keys_row.rearrange("(j r e) -> r j e", j=4, e=EP), key_t.rearrange("p (j e) -> p j e", j=4)).then_inc(S["key_out"], 16)
            sp.wait_ge(S["key_out"], 16)

            def rows_dma(n, r):
                if not (isinstance(n, int) and n < 2):
                    sp.wait_ge(S["rows_used"], RB * (n - 1))
                start = n * RB * EP
                part = keys_row[start:start + RB * EP] if isinstance(n, int) else keys_row[ds(start, RB * EP)]
                sp.dma_start(rows[:, r, :, :].rearrange("p m e -> p (m e)"), part.partition_broadcast(EP)).then_inc(S[f"rows_in{r}"], 16)

            rows_dma(0, 0)
            rows_dma(1, 1)
            with sp.Fori(1, EC // RB // 2) as n:
                rows_dma(n * 2, 0)
                rows_dma(n * 2 + 1, 1)
            sp.wait_ge(S["x1_done"], NTT)
            with nc.allow_non_contiguous_dma(reason="a few hundred bias words, once"):
                for to, a in ((f1b[:, :], f1_b.rearrange("(f p) -> p f", p=128)), (bih[:, :], b_ih.rearrange("(f p) -> p f", p=128)),
                              (bhh[:, :], b_hh.rearrange("(f p) -> p f", p=128)), (Wgs[:, :, :], Wg.rearrange("(c p) e -> p c e", p=128)),
                              (b2s[:, :], b2), (gb[:, 0, :], bg.partition_broadcast(NT)), (gb[:, 1, :], gbias.partition_broadcast(NT))):
                    sp.dma_start(to, a).then_inc(S["d_small"], 16)
                sp.dma_start(b1s[:, :, :].rearrange("p e f -> p (e f)"), b1.rearrange("e (f p) -> p (e f)", p=128)).then_inc(S["d_small"], 16)
            for to, a in ((Ow, O_w), (F1, f1_w), (F2, f2_w), (Wih, w_ih), (Whh, w_hh)):
                sp.dma_start(to, a.rearrange("(c p) d -> p c d", p=128)).then_inc(S["dw_in"], 16)
            for v, a in enumerate((O_b, ln1_w, ln1_b, f2_b, ln2_w, ln2_b)):
                sp.dma_start(vecs[:, v, :], a.partition_broadcast(NT)).then_inc(S["dw_in"], 16)
            sp.wait_ge(S["scattered"], 16 * EC)
            def att_store(b):
                sp.wait_ge(S["aggm"], b + 1)
                sp.dma_start(att_rows[b, :, :], attb[b % 2].rearrange("p t d -> p (t d)")).then_inc(S[f"att_out{b % 2}"], 16)

            cnt_v = counts[0:CELLS, :].rearrange("(k p n) o -> p k (n o)", p=NT, n=NP)
            for b in range(NB):
                if b >= 2:
                    sp.wait_ge(S["agg"], b - 1)
                sp.dma_start(slab[b % 2], cnt_v[:, :, b * QB:(b + 1) * QB]).then_inc(S[f"slab_in{b % 2}"], 16)
                if b >= 2:
                    att_store(b - 2)
            att_store(NB - 2)
            att_store(NB - 1)
            sp.wait_ge(S["agg"], NB)
            for e in range(NE):
                sp.dma_start(W1s[:, e, :, :], W1[e, :, :].rearrange("(c p) f -> p c f", p=128)).then_inc(S["moe_in"], 16)
                sp.dma_start(W2s[:, e, :, :], W2[e, :, :].rearrange("(c p) f -> p c f", p=128)).then_inc(S["moe_in"], 16)

            sp.wait_ge(S["att_out0"], 16 * (NB - NB // 2))
            sp.wait_ge(S["att_out1"], 16 * (NB // 2))

            def d_in(b):
                sp.dma_start(h.rearrange("p t d -> p (t d)"), att_rows[b, :, :] if isinstance(b, int) else att_rows[ds(b, 1), :, :].rearrange("a p d -> (a p) d")).then_inc(S["d_x"], 16)
                if isinstance(b, int):
                    full = (T - 1) * NT
                    sp.dma_start(xd[:, 0:T - 1, :], x[b * QB:b * QB + full, :].rearrange("(t p) d -> p t d", p=NT)).then_inc(S["d_x"], 16)
                    sp.dma_start(xd[0:LROWS, T - 1, :], x[b * QB + full:N, :]).then_inc(S["d_x"], 16)
                else:
                    sp.dma_start(xd, x[ds(b * QB, QB), :].rearrange("(t p) d -> p t d", p=NT)).then_inc(S["d_x"], 16)

            def d_outp(b):
                sp.wait_ge(S["d_acc"], (b + 1) * NE)
                if isinstance(b, int):
                    full = (T - 1) * NT
                    sp.dma_start(out[b * QB:b * QB + full, :].rearrange("(t p) d -> p t d", p=NT), acc[:, 0:T - 1, :]).then_inc(S["d_out"], 16)
                    sp.dma_start(out[b * QB + full:N, :], acc[0:LROWS, T - 1, :]).then_inc(S["d_out"], 16)
                else:
                    sp.dma_start(out[ds(b * QB, QB), :].rearrange("(t p) d -> p t d", p=NT), acc).then_inc(S["d_out"], 16)

            with sp.Fori(0, NB - 1) as b:
                d_in(b)
                d_outp(b)
            d_in(NB - 1)
            d_outp(NB - 1)
            sp.wait_ge(S["d_out"], 16 * (NB + 1))

        @block.gpsimd
        def _(pool):
            nc.gpsimd.memset(halfneg[:, :], -0.5).then_inc(S["consts"], 1)
            nc.gpsimd.memset(ident[:, :], 0.0).then_inc(S["consts"], 1)
            nc.gpsimd.memset(first_w[:, :], 257.0).then_inc(S["consts"], 1)
            pool.wait_ge(S["consts"], 3)
            nc.gpsimd.affine_select(out=ident[:, :], in_=ident[:, :], compare_op=ALU.not_equal, fill=1.0, base=0,
                                    pattern=[[-1, 128]], channel_multiplier=1).then_inc(S["consts"], 1)
            nc.gpsimd.affine_select(out=first_w[:, :], in_=first_w[:, :], compare_op=ALU.is_gt, fill=1.0, base=0,
                                    pattern=[[-1, EP]], channel_multiplier=1).then_inc(S["consts"], 1)
            nc.gpsimd.iota(spare[:, :], pattern=[[0, 1]], base=CELLS, channel_multiplier=1,
                           allow_small_or_imprecise_dtypes=True).then_inc(S["consts"], 1)
            nc.gpsimd.iota(iota8[:, :], pattern=[[1, NE]], base=0, channel_multiplier=0,
                           allow_small_or_imprecise_dtypes=True).then_inc(S["consts"], 1)
            for b in range(NB):
                pool.wait_ge(S["mv_done"], T * (b + 1))
                nc.gpsimd.tensor_scalar(ve[:, :], mean_var[:, T * b:T * b + T, 1], EPS, None, ALU.add).then_inc(S["pool_ve"], 1)
                pool.wait_ge(S["pool_ve"], b + 1)
                nc.gpsimd.tensor_tensor(rstd[:, T * b:T * b + T], ve[:, :], halfneg[:, :], ALU.pow).then_inc(S["rstd_done"], 1)
            pool.wait_ge(S["rstd_done"], NB)
            pool.wait_ge(S["zeroed"], 16 * (NTT + 1))
            with pool.Fori(0, EC // EB) as j:
                pool.wait_ge(S["targets"], j + 1)
                pool.nop(nofuse=True)
                nc.gpsimd.tensor_copy(sc_idx[:, :], target[:, ds(j * EB, EB)]).then_inc(S["sc_copied"], 1)
                nc.gpsimd.tensor_copy(sc_val[:, :], tally[:, ds(j * EB, EB)]).then_inc(S["sc_copied"], 1)
                pool.wait_ge(S["sc_copied"], j * 2 + 2)
                pool.nop(nofuse=True)
                for m in range(EB):
                    pool.indirect_dma_start(counts, bass.IndirectOffsetOnAxis(ap=sc_idx[:, m:m + 1], axis=0), sc_val[:, m:m + 1], None,
                                            compute_op=ALU.add).then_inc(S["scattered"], 16)
                    pool.wait_ge(S["scattered"], j * (16 * EB) + 16 * (m + 1))
                    pool.nop(nofuse=True)

            def d_rstd(n):
                pool.wait_ge(S["d_mv"], n + 1)
                pool.nop(nofuse=True)
                nc.gpsimd.tensor_scalar(dve_[:, :], dmv[:, :, 1], EPS, None, ALU.add).then_inc(S["d_ve"], 1)
                pool.wait_ge(S["d_ve"], n + 1)
                pool.nop(nofuse=True)
                nc.gpsimd.tensor_tensor(drs[:, :], dve_[:, :], halfneg[:, :], ALU.pow).then_inc(S["d_rs"], 1)

            with pool.Fori(0, NB * 3) as n:
                d_rstd(n)

        @block.scalar
        def _(act):
            act.wait_ge(S["zeros_set"], 1)
            cells = counts[0:CELLS, :].rearrange("(k p a n) o -> k p a (n o)", k=NTT, p=NT, a=4)
            for k in range(NTT):
                act.dma_start(cells[k, :, :, :], zeros[:, :].unsqueeze(1).to_broadcast([NT, 4, NP // 4])).then_inc(S["zeroed"], 16)
            act.dma_start(counts[CELLS:CELLS + 128, :].rearrange("(p a) o -> p (a o)", a=2), zeros[0:64, 0:2]).then_inc(S["zeroed"], 16)

            def heads(i):
                act.wait_ge(S["sc_done"], i + 1)
                nc.scalar.activation(probs[:, i % 2, :], shifted_s[:, i % 2, :], ACT.Exp, scale=SCALE).then_inc(S["ex_done"], 1)

            for b in range(NB):
                act.wait_ge(S["tr_done"], b + 1)
                if b >= 2:
                    act.wait_ge(S["proj"], T * (b - 1))
                nc.scalar.copy(xnT[:, b % 2, :, :], pair[b % 2][:, :, 0:QB]).then_inc(S["tr_act"], 1)
                for t in range(T):
                    i = T * b + t
                    act.wait_ge(S["proj"], i + 1)
                    if i >= 2:
                        act.wait_ge(S["x1_done"], i - 1)
                    nc.scalar.copy(qkv[:, i % 2, :], pair[2 + i % 2][0:NT, :, :].rearrange("p a n -> p (a n)")[:, 0:3 * D]).then_inc(S["qkv_done"], 1)
                    if i >= 1:
                        heads(i - 1)
            heads(NTT - 1)

            act.wait_ge(S["d_small"], 16 * 8)
            act.wait_ge(S["dw_prep"], 3)

            def d_block(b):
                def t_copy(n):
                    act.wait_ge(S["d_hT"], b * 4 + n + 1)
                    nc.scalar.copy(attB if n == 0 else hT, pair[1][:, :, 0:QB]).then_inc(S["d_hTe"], 1)

                t_copy(0)
                t_copy(1)
                act.wait_ge(S["d_f1"], b + 1)
                for f in range(FT):
                    nc.scalar.activation(hid[0][:, f, :], bank[4 + f][:, 0:QB], ACT.Relu, bias=f1b[:, f:f + 1]).then_inc(S["d_fT"], 1)
                t_copy(2)
                act.wait_ge(S["d_g"], b + 1)
                for m in range(C):
                    nc.scalar.activation(rT[:, m, :], pair[0][:, m, 0:QB], ACT.Tanh, bias=brz[:, m:m + 1], scale=0.5).then_inc(S["d_tr"], 1)
                for m in range(C):
                    nc.scalar.activation(zT[:, m, :], pair[1][:, m, 0:QB], ACT.Tanh, bias=brz[:, C + m:C + m + 1], scale=0.5).then_inc(S["d_tr"], 1)
                act.wait_ge(S["d_w"], b + 1)
                for m in range(C):
                    nc.scalar.activation(nT[:, m, :], uT[:, m, :], ACT.Tanh, bias=bih[:, 4 + m:5 + m]).then_inc(S["d_n"], 1)
                t_copy(3)
                act.wait_ge(S["d_dd"], b + 1)
                nc.scalar.activation(eg[:, :], gap[:, :], ACT.Exp).then_inc(S["d_ex"], 1)
                act.wait_ge(S["d_cT"], b + 1)
                nc.scalar.copy(combT[:, :], bank[5][0:NE, 0:QB]).then_inc(S["d_cTe"], 1)
                for e in range(NE):
                    for f in range(ET):
                        act.wait_ge(S["d_h1"], b * (NE * ET) + e * ET + f + 1)
                        if e >= 2 and f == 0:
                            act.wait_ge(S["d_ye"], b * NE + e - 1)
                        nc.scalar.activation(hid[e % 2][:, f, :], bank[4 + f][:, 0:QB], ACT.Relu, bias=b1s[:, e, f:f + 1]).then_inc(S["d_he"], 1)

            with act.Fori(0, NB) as b:
                d_block(b)

        @block.vector
        def _(dve):
            nlink = [0]

            def link(ins):
                nlink[0] += 1
                ins.then_inc(S["chain"], 1)
                dve.wait_ge(S["chain"], nlink[0])

            nc.vector.memset(zeros[:, :], 0.0).then_inc(S["zeros_set"], 1)
            nc.vector.memset(x_in[:, NB - 1, T - 1, :], 0.0).then_inc(S["zeros_set"], 1)
            dve.wait_ge(S["e_in"], 32)
            nc.vector.scalar_tensor_tensor(key[:, :], src_i, float(NP), dst_i, ALU.mult, ALU.add).then_inc(S["key_done"], 1)
            def heads_scores(i):
                r = i % 2
                dve.wait_ge(S["qkv_done"], i + 1)
                q_ = qkv[:, r, 0:D].rearrange("p (h d) -> p h d", h=H).unsqueeze(2).to_broadcast([NT, H, H, DH])
                k_ = qkv[:, r, D:2 * D].rearrange("p (g d) -> p g d", g=H).unsqueeze(1).to_broadcast([NT, H, H, DH])
                link(nc.vector.tensor_tensor(prod.rearrange("p (h g d) -> p h g d", h=H, g=H), q_, k_, ALU.mult))
                link(nc.vector.tensor_reduce(scores, prod.rearrange("p (a d) -> p a d", d=DH), AX, ALU.add))
                link(nc.vector.tensor_reduce(hmax, scores.rearrange("p (h g) -> p h g", h=H), AX, ALU.max))
                nc.vector.tensor_tensor(shifted_s[:, r, :].rearrange("p (h g) -> p h g", h=H), scores.rearrange("p (h g) -> p h g", h=H),
                                        hmax.unsqueeze(2).to_broadcast([NT, H, H]), ALU.subtract).then_inc(S["sc_done"], 1)

            def heads_out(i):
                r = i % 2
                pr = probs[:, r, :].rearrange("p (h g) -> p h g", h=H)
                dve.wait_ge(S["ex_done"], i + 1)
                link(nc.vector.tensor_reduce(hsum, pr, AX, ALU.add))
                link(nc.vector.reciprocal(hinv, hsum))
                link(nc.vector.tensor_tensor(pr, pr, hinv.unsqueeze(2).to_broadcast([NT, H, H]), ALU.mult))
                v_ = qkv[:, r, 2 * D:3 * D].rearrange("p (g d) -> p d g", g=H)
                for h_ in range(H):
                    ins = nc.vector.tensor_tensor(prod.rearrange("p (h d g) -> p h d g", h=H, g=H)[:, h_, :, :], v_,
                                                  pr[:, h_:h_ + 1, :].to_broadcast([NT, DH, H]), ALU.mult)
                link(ins)
                nc.vector.tensor_reduce(x1[:, i, :], prod.rearrange("p (a g) -> p a g", g=H), AX, ALU.add).then_inc(S["x1_done"], 1)
                dve.wait_ge(S["x1_done"], i + 1)

            def ln_block(b):
                r = b % 2
                dve.wait_ge(S[f"x_in{b}"], 32 if b == NB - 1 else 16)
                for t in range(T):
                    nc.vector.bn_stats(stats[:, t, :], x_in[:, b, t, :]).then_inc(S["st_done"], 1)
                dve.wait_ge(S["st_done"], T * (b + 1))
                for t in range(T):
                    nc.vector.bn_aggr(mean_var[:, T * b + t, :], stats[:, t, :]).then_inc(S["mv_done"], 1)
                dve.wait_ge(S["mv_done"], T * (b + 1))
                if b == 0:
                    dve.wait_ge(S["key_tr"], 1)
                    nc.vector.tensor_copy(key_t, bank[7][0:EC // 4, 0:4 * EP]).then_inc(S["key_row"], 1)
                if b >= 2:
                    dve.wait_ge(S["tr_done"], b - 1)
                dve.wait_ge(S["rstd_done"], b + 1)
                for t in range(T):
                    i = T * b + t
                    nc.vector.tensor_scalar(x_ln[:, r, t, :], x_in[:, b, t, :], mean_var[:, i, 0:1], rstd[:, i:i + 1],
                                            ALU.subtract, ALU.mult).then_inc(S["ln_done"], 1)

            ln_block(0)
            ln_block(1)

            def col(t, c, w=1):
                return t[:, c:c + w] if isinstance(c, int) else t[:, ds(c, w)]

            def edge(c, n, r, m):
                if m == 0:
                    dve.wait_ge(S[f"rows_in{r}"], 16 * n)
                if not (isinstance(c, int) and c == 0):
                    dve.wait_ge(S["rows_used"], c)
                nc.vector.scalar_tensor_tensor(eq[:, :], rows[:, r, m, :], col(key, c), first_w[:, :], ALU.is_equal, ALU.mult,
                                               accum_out=col(tally, c)).then_inc(S["rows_used"], 1)

            def edge_targets(c, used, links):
                dve.wait_ge(S["rows_used"], used)
                nc.vector.tensor_scalar(fresh[:, :], col(tally, c, EB), 256.0, None, ALU.is_lt).then_inc(S["chain"], 1)
                dve.wait_ge(S["chain"], links + 1)
                nc.vector.scalar_tensor_tensor(shifted[:, :], col(key, c, EB), spare[:, 0:1], fresh[:, :], ALU.subtract, ALU.mult).then_inc(S["chain"], 1)
                dve.wait_ge(S["chain"], links + 2)
                nc.vector.tensor_scalar(col(target, c, EB), shifted[:, :], spare[:, 0:1], None, ALU.add).then_inc(S["targets"], 1)

            dve.wait_ge(S["consts"], 7)

            def edges_of(c0, n):
                for c in range(c0, c0 + n):
                    edge(c, c // (2 * RB) + 1, (c // RB) % 2, c % RB)
                    if c % EB == EB - 1:
                        edge_targets(c + 1 - EB, c + 1, nlink[0])
                        nlink[0] += 2

            edges_of(0, 2 * EB)
            for b in range(NB):
                for t in range(T):
                    heads_scores(T * b + t)
                    if T * b + t >= 1:
                        heads_out(T * b + t - 1)
                if b + 2 < NB:
                    ln_block(b + 2)
                edges_of(2 * EB + b * 40, 40)
            heads_out(NTT - 1)
            edges_of(2 * EB + NB * 40, EC - 2 * EB - NB * 40)

            for b in range(NB):
                dve.wait_ge(S["agg"], b + 1)
                if b >= 2:
                    dve.wait_ge(S[f"att_out{b % 2}"], 16 * (b // 2))
                nc.vector.tensor_tensor(attb[b % 2], x1[:, T * b:T * b + T, :], pair[2 + b % 2][0:NT, :, :].rearrange("p a (u d) -> p (a u) d", u=2), ALU.mult).then_inc(S["aggm"], 1)
            dve.wait_ge(S["dw_in"], 16 * 11)
            dve.wait_ge(S["d_small"], 16 * 8)
            nc.vector.tensor_tensor(Wih[:, :, 0:2 * D], Wih[:, :, 0:2 * D], Whh[:, :, 0:2 * D], ALU.add).then_inc(S["dw_prep"], 1)
            nc.vector.tensor_tensor(gb[:, 0, :], gb[:, 0, :], gb[:, 1, :], ALU.add).then_inc(S["dw_prep"], 1)
            link(nc.vector.tensor_tensor(brz[:, :], bih[:, 0:4], bhh[:, 0:4], ALU.add))
            nc.vector.tensor_scalar(brz[:, :], brz[:, :], 0.5, None, ALU.mult).then_inc(S["dw_prep"], 1)
            dve.wait_ge(S["dw_prep"], 3)
            d_base = nlink[0]
            D_LINKS = 25

            def d_block(b, xn):
                cnt = [0]

                def dl(ins):
                    cnt[0] += 1
                    ins.then_inc(S["chain"], 1)
                    dve.wait_ge(S["chain"], b * D_LINKS + (d_base + cnt[0]))

                def bc(v):
                    return vecs[:, v:v + 1, :].to_broadcast([NT, T, D])

                s0 = pair[0][0:NT, :, :].rearrange("p a (u d) -> p (a u) d", u=2)

                def ln(n, src_, dst_):
                    for t in range(T):
                        last = nc.vector.bn_stats(stats[:, t, :], src_[:, t, :])
                    dl(last)
                    dve.nop(nofuse=True)
                    for t in range(T):
                        last = nc.vector.bn_aggr(dmv[:, t, :], stats[:, t, :])
                    last.then_inc(S["d_mv"], 1)
                    dve.wait_ge(S["d_rs"], b * 3 + n + 1)
                    for t in range(T):
                        last = nc.vector.tensor_scalar(dst_[:, t, :], src_[:, t, :], dmv[:, t, 0:1], drs[:, t:t + 1], ALU.subtract, ALU.mult)
                    return last

                dve.wait_ge(S["d_x"], b * 32 + (48 if isinstance(b, int) else 32))
                dve.wait_ge(S["d_ho"], b + 1)
                mvb = mean_var[:, :, :].rearrange("p i v -> p (i v)")
                for t in range(T):
                    last = nc.vector.tensor_scalar(h[:, t, :], xd[:, t, :], col(mvb, b * (2 * T) + 2 * t), col(rstd, b * T + t), ALU.subtract, ALU.mult)
                dl(last)
                dve.wait_ge(S["d_ho"], b + 1)
                dl(nc.vector.tensor_tensor(h, h, s0, ALU.add))
                dl(nc.vector.tensor_tensor(h, h, bc(0), ALU.add))
                dl(ln(0, h, h))
                dl(nc.vector.tensor_tensor(h, h, bc(1), ALU.mult))
                nc.vector.tensor_tensor(h, h, bc(2), ALU.add).then_inc(S["d_h"], 1)
                dve.wait_ge(S["d_h"], b * 2 + 1)
                dve.wait_ge(S["d_f2"], b + 1)
                dl(nc.vector.tensor_tensor(h, h, s0, ALU.add))
                dl(nc.vector.tensor_tensor(h, h, bc(3), ALU.add))
                dl(ln(1, h, h))
                dl(nc.vector.tensor_tensor(h, h, bc(4), ALU.mult))
                nc.vector.tensor_tensor(h, h, bc(5), ALU.add).then_inc(S["d_h"], 1)
                dve.wait_ge(S["d_g"], b + 1)
                for m in range(C):
                    last = nc.vector.tensor_scalar(uT[:, m, :], pair[3][:, m, 0:QB], bhh[:, 4 + m:5 + m], None, ALU.add)
                dl(last)
                dve.wait_ge(S["d_tr"], (b + 1) * 4)
                dl(nc.vector.scalar_tensor_tensor(uT, rT, 1.0, uT, ALU.add, ALU.mult))
                for m in range(C):
                    last = nc.vector.scalar_tensor_tensor(uT[:, m, :], uT[:, m, :], 0.5, bank[4 + m][:, 0:QB], ALU.mult, ALU.add)
                last.then_inc(S["d_w"], 1)
                dve.wait_ge(S["d_n"], (b + 1) * 2)
                dl(nc.vector.tensor_tensor(uT, hT, nT, ALU.subtract))
                dl(nc.vector.scalar_tensor_tensor(uT, zT, 1.0, uT, ALU.add, ALU.mult))
                nc.vector.scalar_tensor_tensor(uT, uT, 0.5, nT, ALU.mult, ALU.add).then_inc(S["d_gT"], 1)
                dve.wait_ge(S["d_gn"], b + 1)
                dl(nc.vector.tensor_tensor(x2, xd, s0, ALU.add))
                ln(2, x2, h).then_inc(S["d_y"], 1)
                dve.wait_ge(S["d_lg"], b + 1)
                dl(nc.vector.tensor_tensor(lg[:, :, :], bank[4][0:NT, 0:T * NE].rearrange("p (t e) -> p t e", t=T), gb[:, 0:1, :].to_broadcast([NT, T, NE]), ALU.add))
                dve.nop(nofuse=True)
                for t in range(T):
                    last = nc.vector.max(top[:, t, :], lg[:, t, :])
                dl(last)
                dve.nop(nofuse=True)
                for t in range(T):
                    last = nc.vector.max_index(topi[:, t, :], top[:, t, :], lg[:, t, :])
                dl(last)
                nc.vector.tensor_tensor(gap[:, :], top[:, :, 1], top[:, :, 0], ALU.subtract).then_inc(S["d_dd"], 1)
                dl(nc.vector.tensor_copy(topf[:, :, :], topi[:, :, 0:2]))
                for j in range(2):
                    last = nc.vector.tensor_tensor(oh[:, j, :, :], iota8[:, :].unsqueeze(1).to_broadcast([NT, T, NE]),
                                                   topf[:, :, j:j + 1].to_broadcast([NT, T, NE]), ALU.is_equal)
                dve.wait_ge(S["d_ex"], b + 1)
                dl(nc.vector.tensor_scalar(w1[:, :], eg[:, :], 1.0, None, ALU.add))
                dl(nc.vector.reciprocal(w1[:, :], w1[:, :]))
                dl(nc.vector.tensor_tensor(w2[:, :], eg[:, :], w1[:, :], ALU.mult))
                for j, w in enumerate((w1, w2)):
                    last = nc.vector.tensor_tensor(oh[:, j, :, :], oh[:, j, :, :], w[:, :].unsqueeze(2).to_broadcast([NT, T, NE]), ALU.mult)
                dl(last)
                nc.vector.tensor_tensor(comb[:, :, :], oh[:, 0, :, :], oh[:, 1, :, :], ALU.add).then_inc(S["d_comb"], 1)
                dve.wait_ge(S["d_b2"], b + 1)
                if isinstance(b, int):
                    dve.wait_ge(S["d_out"], 16 * b)
                else:
                    dve.wait_ge(S["d_out"], b * 16)
                nc.vector.tensor_tensor(acc, x2, s0, ALU.add).then_inc(S["d_acc0"], 1)
                dve.wait_ge(S["d_acc0"], b + 1)
                for e in range(NE):
                    dve.wait_ge(S["d_ye"], b * NE + e + 1)
                    se = pair[(e + 1) % 2][0:NT, :, :].rearrange("p a (u d) -> p (a u) d", u=2)
                    for t in range(T):
                        last = nc.vector.scalar_tensor_tensor(acc[:, t, :], se[:, t, :], comb[:, t, e:e + 1], acc[:, t, :], ALU.mult, ALU.add)
                    last.then_inc(S["d_acc"], 1)
                    dve.wait_ge(S["d_acc"], b * NE + e + 1)
                assert cnt[0] == D_LINKS, cnt[0]

            with dve.Fori(0, NB - 1) as b:
                d_block(b, None)
            d_block(NB - 1, None)

        @block.tensor
        def _(pe):
            pe.wait_ge(S["consts"], 4)
            pe.wait_ge(S["key_done"], 1)
            q = EC // 4
            for j in range(4):
                last = nc.tensor.transpose(bank[7][0:q, j * EP:(j + 1) * EP], key[:, j * q:(j + 1) * q], ident[0:EP, 0:EP])
            last.then_inc(S["key_tr"], 1)
            for b in range(NB):
                pe.wait_ge(S["ln_done"], T * (b + 1))
                if b >= 2:
                    pe.wait_ge(S["tr_act"], b - 1)
                for c in range(C):
                    for t in range(T):
                        last = nc.tensor.transpose(bank[2 * (b % 2) + c][:, t * NT:(t + 1) * NT], x_ln[:, b % 2, t, c * 128:(c + 1) * 128], ident[0:NT, 0:NT])
                last.then_inc(S["tr_done"], 1)
                pe.wait_ge(S["w_in"], 48)
                pe.wait_ge(S["key_row"], 1)
                pe.wait_ge(S["tr_act"], b + 1)
                for t in range(T):
                    i = T * b + t
                    if i >= 2:
                        pe.wait_ge(S["qkv_done"], i - 1)
                    for lo, hi in ((0, SPLIT), (SPLIT, 3 * D)):
                        for c in range(C):
                            last = nc.tensor.matmul(pair[2 + i % 2][0:NT, lo // SPLIT, 0:hi - lo], xnT[:, b % 2, c, t * NT:(t + 1) * NT], wqkv[:, c, lo:hi],
                                                    start=(c == 0), stop=(c == C - 1))
                    last.then_inc(S["proj"], 1)

            pe.wait_ge(S["x1_done"], NTT)

            def aggregate(b):
                for t in range(T):
                    for k in range(NTT):
                        last = nc.tensor.matmul(bank[4 + 2 * (b % 2) + t // 2][0:NT, (t % 2) * D:(t % 2 + 1) * D], slab[b % 2][:, k, t * NT:(t + 1) * NT], x1[:, k, :],
                                                start=(k == 0), stop=(k == NTT - 1))
                last.then_inc(S["agg"], 1)

            for b in range(NB):
                pe.wait_ge(S[f"slab_in{b % 2}"], 16 * (b // 2 + 1))
                if b >= 2:
                    pe.wait_ge(S["aggm"], b - 1)
                aggregate(b)
            pe.wait_ge(S["dw_prep"], 3)
            pe.wait_ge(S["moe_in"], 16 * 2 * NE)

            def d_block(b):
                s0 = pair[0][0:NT, :, :].rearrange("p a (u d) -> p (a u) d", u=2)

                def by_rows(dst_, lhsT, rhs, steps, done):
                    for t in range(T):
                        for c in range(steps):
                            last = nc.tensor.matmul(dst_[:, t, :], lhsT[:, c, t * NT:(t + 1) * NT], rhs[:, c, :], start=(c == 0), stop=(c == steps - 1))
                    last.then_inc(S[done], 1)

                def turned(src_):
                    for c in range(C):
                        for t in range(T):
                            last = nc.tensor.transpose(pair[1][:, c, t * NT:(t + 1) * NT], src_[:, t, c * 128:(c + 1) * 128], ident[0:NT, 0:NT])
                    last.then_inc(S["d_hT"], 1)

                pe.wait_ge(S["d_x"], b * 32 + (48 if isinstance(b, int) else 32))
                turned(h)
                pe.wait_ge(S["d_hTe"], b * 4 + 1)
                by_rows(s0, attB, Ow, C, "d_ho")
                pe.wait_ge(S["d_h"], b * 2 + 1)
                turned(h)
                pe.wait_ge(S["d_hTe"], b * 4 + 2)
                for f in range(FT):
                    for c in range(C):
                        last = nc.tensor.matmul(bank[4 + f][:, 0:QB], F1[:, c, f * 128:(f + 1) * 128], hT[:, c, :], start=(c == 0), stop=(c == C - 1))
                last.then_inc(S["d_f1"], 1)
                pe.wait_ge(S["d_fT"], (b + 1) * FT)
                by_rows(s0, hid[0], F2, FT, "d_f2")
                pe.wait_ge(S["d_h"], b * 2 + 2)
                turned(h)
                pe.wait_ge(S["d_hTe"], b * 4 + 3)
                for m in range(3 * C):
                    to = bank[m]
                    for c in range(C):
                        nc.tensor.matmul(to[:, 0:QB], Wih[:, c, m * 128:(m + 1) * 128], hT[:, c, :], start=(c == 0), stop=(c == C - 1))
                for m in range(C):
                    for c in range(C):
                        last = nc.tensor.matmul(pair[3][:, m, 0:QB], Whh[:, c, (2 * C + m) * 128:(2 * C + m + 1) * 128], hT[:, c, :], start=(c == 0), stop=(c == C - 1))
                last.then_inc(S["d_g"], 1)
                pe.wait_ge(S["d_gT"], b + 1)
                for t in range(T):
                    for c in range(C):
                        last = nc.tensor.transpose(s0[:, t, c * 128:(c + 1) * 128], uT[:, c, t * NT:(t + 1) * NT], ident[:, :])
                last.then_inc(S["d_gn"], 1)
                pe.wait_ge(S["d_y"], b + 1)
                turned(h)
                pe.wait_ge(S["d_hTe"], b * 4 + 4)
                for t in range(T):
                    for c in range(C):
                        last = nc.tensor.matmul(bank[4][0:NT, t * NE:(t + 1) * NE], hT[:, c, t * NT:(t + 1) * NT], Wgs[:, c, :], start=(c == 0), stop=(c == C - 1))
                last.then_inc(S["d_lg"], 1)
                pe.wait_ge(S["d_comb"], b + 1)
                for t in range(T):
                    last = nc.tensor.transpose(bank[5][0:NE, t * NT:(t + 1) * NT], comb[:, t, :], ident[0:NT, 0:NT])
                last.then_inc(S["d_cT"], 1)
                pe.wait_ge(S["d_cTe"], b + 1)
                for t in range(T):
                    last = nc.tensor.matmul(s0[:, t, :], combT[:, t * NT:(t + 1) * NT], b2s[:, :], start=True, stop=True)
                last.then_inc(S["d_b2"], 1)

                def up(e):
                    for f in range(ET):
                        if e >= 1:
                            pe.wait_ge(S["d_he"], b * (NE * ET) + (e - 1) * ET + f + 1)
                        for c in range(C):
                            last = nc.tensor.matmul(bank[4 + f][:, 0:QB], W1s[:, e, c, f * 128:(f + 1) * 128], hT[:, c, :], start=(c == 0), stop=(c == C - 1))
                        last.then_inc(S["d_h1"], 1)

                up(0)
                for e in range(NE):
                    if e + 1 < NE:
                        up(e + 1)
                    pe.wait_ge(S["d_he"], b * (NE * ET) + (e + 1) * ET)
                    if e == 1:
                        pe.wait_ge(S["d_acc0"], b + 1)
                    if e >= 2:
                        pe.wait_ge(S["d_acc"], b * NE + e - 1)
                    by_rows(pair[(e + 1) % 2][0:NT, :, :].rearrange("p a (u d) -> p (a u) d", u=2), hid[e % 2], W2s[:, e, :, :], ET, "d_ye")

            with pe.Fori(0, NB - 1) as b:
                d_block(b)
            d_block(NB - 1)


_INS = ['x', 'src', 'dst'] + ['L0_gnn_' + n for n in ('Wq', 'Wk', 'Wv', 'O_w', 'O_b', 'ln1_w', 'ln1_b', 'f1_w', 'f1_b', 'f2_w', 'f2_b',
        'ln2_w', 'ln2_b', 'gru_w_ih', 'gru_w_hh', 'gru_b_ih', 'gru_b_hh')] + ['L0_ffn_' + n for n in ('Wg', 'bg', 'bias', 'W1', 'b1', 'W2', 'b2')]


def kernel(**inputs):
    import numpy as _np
    import concourse.bacc as _bacc
    from concourse import mybir as _mybir
    from concourse.bass_utils import run_bass_kernel_spmd as _run

    nc = _bacc.Bacc("TRN2", target_bir_lowering=False, num_devices=1)
    arrays, args = {}, []
    for name in _INS:
        a = _np.ascontiguousarray(inputs[name])
        arrays[f"in_{name}_dram"] = a
        args.append(nc.dram_tensor(f"in_{name}_dram", a.shape, _mybir.dt.from_np(a.dtype), kind="ExternalInput").ap())
    args.append(nc.dram_tensor("out_0_dram", inputs["x"].shape, _mybir.dt.float32, kind="ExternalOutput").ap())
    gnn_moe_layer(nc, *args)
    r = _run(nc, [arrays], core_ids=[0])
    return r.results[0]["out_0_dram"]
```

```python
import concourse.bass as bass
from concourse import mybir
from contextlib import ExitStack


def gnn_moe_layer(nc, x, src, dst, Wq, Wk, Wv, O_w, O_b, ln1_w, ln1_b, f1_w, f1_b, f2_w, f2_b,
                  ln2_w, ln2_b, w_ih, w_hh, b_ih, b_hh, Wg, bg, gbias, W1, b1, W2, b2, out):
    f32, f16, i32, u32 = mybir.dt.float32, mybir.dt.float16, mybir.dt.int32, mybir.dt.uint32
    ALU, ACT, AX = mybir.AluOpType, mybir.ActivationFunctionType, mybir.AxisListType.X
    ds = bass.ds

    N, D = x.shape
    C = D // 128
    H, DH = 8, 32
    HG = 128 // DH
    G = H // HG
    QB = 448
    NB = -(-N // QB)
    NP = NB * QB
    T = 4
    NT = QB // T
    E = src.shape[0]
    EK = 4
    EG = -(-E // (EK * 128))
    ELAST = E - (EG - 1) * EK * 128
    RING = 8
    NTT = NB * T
    FAR = 1000000
    SPLIT = 512
    F = f1_w.shape[1]
    FT = F // 128
    NE, FE = W1.shape[0], W1.shape[2]
    ET = FE // 128
    SCALE = float(DH) ** -0.5
    EPS = 1e-5
    LAST = N - (NB - 1) * QB
    LROWS = LAST - (T - 1) * NT

    x1_rows = nc.dram_tensor("x1_rows", (NP, D), f32, kind="Internal").ap()

    ctx = ExitStack()
    with ctx:
        def sb(name, shape, dt=f32):
            return ctx.enter_context(nc.sbuf_tensor(name, shape, dt))

        def sem(name):
            return ctx.enter_context(nc.semaphore(name))

        WB = sb("WB", [128, NE * C * FE + NE * ET * D])
        x_in = WB[0:NT, 0:NTT * D].rearrange("p (r t d) -> p r t d", r=NB, t=T)
        o = NTT * D
        x_ln = WB[0:NT, o:o + 2 * T * D].rearrange("p (r t d) -> p r t d", r=2, t=T)
        o += 2 * T * D
        xnT = WB[:, o:o + 2 * C * QB].rearrange("p (r c n) -> p r c n", r=2, c=C)
        o += 2 * C * QB
        qkv = WB[0:NT, o:o + 2 * 3 * D].rearrange("p (r w) -> p r w", r=2)
        o += 2 * 3 * D
        prod = WB[0:NT, o:o + H * H * DH]
        o += H * H * DH
        scores = WB[0:NT, o:o + H * H]
        probs = WB[0:NT, o + 64:o + 192].rearrange("p (r w) -> p r w", r=2)
        shifted_s = WB[0:NT, o + 192:o + 320].rearrange("p (r w) -> p r w", r=2)
        hmax, hsum, hinv = (WB[0:NT, o + 320 + 8 * i:o + 328 + 8 * i] for i in range(3))
        W1s = WB[:, 0:NE * C * FE].rearrange("p (e c f) -> p e c f", e=NE, c=C)
        W2s = WB[:, NE * C * FE:].rearrange("p (e f d) -> p e f d", e=NE, f=ET)

        RB = sb("RB", [128, RING * EK * D])
        x1 = RB[0:NT, 0:NTT * D].rearrange("p (i d) -> p i d", i=NTT)

        WQKV = sb("WQKV", [128, C * 3 * D])
        wqkv = WQKV[:, :].rearrange("p (c w) -> p c w", c=C)
        vecs = WQKV[0:NT, :].rearrange("p (v d) -> p v d", v=6)

        Ow = sb("Ow", [128, C, D])
        F1 = sb("F1", [128, C, F])
        F2 = sb("F2", [128, FT, D])
        Wih = sb("Wih", [128, C, 3 * D])
        Whh = sb("Whh", [128, C, 3 * D])
        f1b = sb("f1b", [128, FT])
        bih = sb("bih", [128, 3 * C])
        bhh = sb("bhh", [128, 3 * C])
        brz = sb("brz", [128, 2 * C])
        b1s = sb("b1s", [128, NE, ET])
        b2s = sb("b2s", [NE, D])
        Wgs = sb("Wgs", [128, C, NE])
        gb = sb("gb", [NT, 2, NE])

        hT = sb("hT", [128, C, QB])
        yT = sb("yT", [128, 2 * C * QB])
        hid = [sb(f"hid{r}", [128, ET, QB]) for r in range(2)]
        h = sb("h", [NT, T, D])
        acc = sb("acc", [NT, 2 * T * D])
        xd = sb("xd", [NT, T, D])
        x1b = sb("x1b", [NT, T, D])
        gates = sb("gates", [128, 4 * C * QB])
        rT, zT, nT, uT = (gates[:, i * C * QB:(i + 1) * C * QB].rearrange("p (c n) -> p c n", c=C) for i in range(4))
        fh = gates[:, 0:FT * QB].rearrange("p (f n) -> p f n", f=FT)
        attT = nT
        edge_i = gates[0:EG, 0:2 * EK * 128].bitcast(i32).rearrange("p (w e) -> p w e", w=2)
        edge_f = gates[0:EG, 2 * EK * 128:4 * EK * 128].rearrange("p (w e) -> p w e", w=2)

        ident = sb("ident", [128, 128])
        mean_var = sb("mean_var", [NT, NTT, 2])
        rstd = sb("rstd", [NT, NTT])
        stats = sb("stats", [NT, T, 6])
        halfneg = sb("halfneg", [NT, T])
        ve = sb("ve", [NT, T])
        eps_t = sb("eps_t", [NT, 1])
        src_tab = sb("src_tab", [128, EG * EK], i32)
        dst_tab = sb("dst_tab", [128, EG * EK])
        idx = sb("idx", [128, RING * EK], i32)
        onehot = [sb(f"onehot{k}", [128, NT]) for k in range(EK)]
        lane = sb("lane", [128, NT])
        tile_neg = sb("tile_neg", [128, NTT])
        tile_lo = sb("tile_lo", [128, NTT])
        group_no = sb("group_no", [NTT, EG])
        dmin = sb("dmin", [EG, 1])
        dmax = sb("dmax", [EG, 1])
        not_above = sb("not_above", [EG, NTT])
        hit = sb("hit", [EG, NTT])
        cand = sb("cand", [NTT, EG])
        cand_hi = sb("cand_hi", [NTT, EG])
        rng = sb("rng", [NTT, 3])
        before = sb("before", [NTT, NTT])
        ranges = sb("ranges", [1, 3 * NTT], i32)
        zrow = sb("zrow", [1, D], f16)
        lg = sb("lg", [NT, T, NE])
        top = sb("top", [NT, T, 8])
        topi = sb("topi", [NT, T, 8], u32)
        topf = sb("topf", [NT, T, 2])
        gap = sb("gap", [NT, T])
        eg = sb("eg", [NT, T])
        w1 = sb("w1", [NT, T])
        w2 = sb("w2", [NT, T])
        oh = sb("oh", [NT, 2, T, NE])
        comb = sb("comb", [NT, T, NE])
        comb_ring = sb("comb_ring", [NT, 2 * T * NE])
        combT = sb("combT", [NE, QB])
        iota8 = sb("iota8", [NT, NE])
        dmv = sb("dmv", [NT, T, 2])
        dsd = sb("dsd", [NT, T])
        drs = sb("drs", [NT, T])

        pair = [ctx.enter_context(nc.psum_tensor(f"pair{i}", [128, 2, 512], f32)) for i in range(4)]
        bank = [pair[i // 2][:, i % 2, :] for i in range(8)]

        def by_nodes(p):
            return pair[p][0:NT, :, :].rearrange("p a (u d) -> p (a u) d", u=2)

        S = {}
        for name in ("w_in x_in0 x_in1 x_in2 x_in3 x_in4 x_in5 x_in6 consts pad_set edges_in edges_f edges_tr tables "
                     "hit_done hit_tr rng_done rng_tr ranges "
                     "st_done mv_done pool_ve rstd_done ln_done tr_done tr_act proj qkv_done sc_done ex_done x1_done x1_out chain "
                     "idx_in rows_ready gath0 gath1 gath2 gath3 gath4 gath5 gath6 gath7 onehot_set row_used agg att "
                     "dw_in d_small dw_prep moe_in1 moe_in2 "
                     "d_x x1b_in d_hT d_hTe d_ho d_mv d_sd d_h d_f1 d_fT d_f2 d_g1 d_g2 d_tr d_u d_w d_n d_gT d_gn d_x2 d_y d_lg "
                     "d_dd d_ex d_comb d_cT d_cTe d_b2 d_acc0 d_h1 d_he d_ye d_acc d_out0 d_out1").split():
            S[name] = sem(name)
        CREDIT = RING * EK

        block = ctx.enter_context(nc.Block())

        def col(t, c, w=1):
            return t[:, c:c + w] if isinstance(c, int) else t[:, ds(c, w)]

        def half(t, b, size):
            return t[:, (b % 2) * size:(b % 2 + 1) * size] if isinstance(b, int) else t[:, ds((b % 2) * size, size)]

        def acc_of(b):
            return half(acc, b, T * D).rearrange("p (t d) -> p t d", t=T)

        def yT_of(b):
            return half(yT, b, C * QB).rearrange("p (c n) -> p c n", c=C)

        def groups_of(eng, i):
            first = eng.value_load(col(ranges, i), min_val=0, max_val=EG - 1)
            count = eng.value_load(col(ranges, NTT + i), min_val=1, max_val=EG)
            done = eng.value_load(col(ranges, 2 * NTT + i), min_val=0, max_val=(NTT - 1) * EG)
            return first, count, done

        def group(first, n):
            return nc.s_assert_within(first + n, 0, EG - 1, skip_runtime_bounds_check_because="a tile's groups end with the last group")

        @block.sync
        def _(sp):
            for b in range(NB):
                if b < NB - 1:
                    sp.dma_start(x_in[:, b, :, :], x[b * QB:(b + 1) * QB, :].rearrange("(t p) d -> p t d", p=NT)).then_inc(S[f"x_in{b}"], 16)
                else:
                    full = (T - 1) * NT
                    sp.wait_ge(S["pad_set"], 3)
                    sp.dma_start(x_in[:, b, 0:T - 1, :], x[b * QB:b * QB + full, :].rearrange("(t p) d -> p t d", p=NT)).then_inc(S[f"x_in{b}"], 16)
                    sp.dma_start(x_in[0:LROWS, b, T - 1, :], x[b * QB + full:N, :]).then_inc(S[f"x_in{b}"], 16)
                if b == 0:
                    for w, a in enumerate((Wq, Wk, Wv)):
                        sp.dma_start(wqkv[:, :, w * D:(w + 1) * D], a.rearrange("(c p) d -> p c d", p=128)).then_inc(S["w_in"], 16)
                    sp.wait_ge(S["pad_set"], 2)
                    whole = (EG - 1) * EK * 128
                    for w, a in enumerate((src, dst)):
                        sp.dma_start(edge_i[0:EG - 1, w, :], a[0:whole].rearrange("(p e) -> p e", p=EG - 1)).then_inc(S["edges_in"], 16)
                        sp.dma_start(edge_i[EG - 1:EG, w, 0:ELAST], a[whole:E].rearrange("(p e) -> p e", p=1)).then_inc(S["edges_in"], 16)
            with nc.allow_non_contiguous_dma(reason="a few hundred bias words, once"):
                for to, a in ((f1b[:, :], f1_b.rearrange("(f p) -> p f", p=128)), (bih[:, :], b_ih.rearrange("(f p) -> p f", p=128)),
                              (bhh[:, :], b_hh.rearrange("(f p) -> p f", p=128)), (Wgs[:, :, :], Wg.rearrange("(c p) e -> p c e", p=128)),
                              (b2s[:, :], b2), (gb[:, 0, :], bg.partition_broadcast(NT)), (gb[:, 1, :], gbias.partition_broadcast(NT))):
                    sp.dma_start(to, a).then_inc(S["d_small"], 16)
                sp.dma_start(b1s[:, :, :].rearrange("p e f -> p (e f)"), b1.rearrange("e (f p) -> p (e f)", p=128)).then_inc(S["d_small"], 16)
            for to, a in ((Ow, O_w), (F1, f1_w), (F2, f2_w), (Wih, w_ih), (Whh, w_hh)):
                sp.dma_start(to[:, :, :], a.rearrange("(c p) d -> p c d", p=128)).then_inc(S["dw_in"], 16)
            for b in range(NB):
                sp.wait_ge(S["x1_done"], T * (b + 1))
                sp.dma_start(x1_rows[b * QB:(b + 1) * QB, :].rearrange("(t p) d -> p t d", p=NT), x1[:, b * T:(b + 1) * T, :]).then_inc(S["x1_out"], 16)
            for v, a in enumerate((O_b, ln1_w, ln1_b, f2_b, ln2_w, ln2_b)):
                sp.dma_start(vecs[:, v, :], a.partition_broadcast(NT)).then_inc(S["dw_in"], 16)
            sp.wait_ge(S["x1_out"], 16 * NB)

            sp.dma_start(xd[:, :, :], x[0:QB, :].rearrange("(t p) d -> p t d", p=NT)).then_inc(S["d_x"], 16)
            sp.dma_start(x1b[:, :, :], x1_rows[0:QB, :].rearrange("(t p) d -> p t d", p=NT)).then_inc(S["x1b_in"], 16)
            sp.wait_ge(S["tables"], 2)
            sp.wait_ge(S["ranges"], 1)
            sp.nop().then_inc(S["idx_in"], 16)
            for e in range(NE):
                sp.dma_start(W1s[:, e, :, :], W1[e, :, :].rearrange("(c p) f -> p c f", p=128)).then_inc(S["moe_in1"], 16)
                sp.dma_start(W2s[:, e, :, :], W2[e, :, :].rearrange("(c p) f -> p c f", p=128)).then_inc(S["moe_in2"], 16)

            def load_indices(u, g):
                sp.wait_ge(S["rows_ready"], u + 1)
                sp.wait_ge(S["idx_in"], u * 16 + 16)
                sp.dma_start(idx[:, ds((u % RING) * EK, EK)], src_tab[:, ds(g * EK, EK)]).then_inc(S["idx_in"], 16)

            with sp.Fori(0, NTT) as i:
                first, count, done = groups_of(sp, i)
                with sp.Fori(0, count) as n:
                    load_indices(done + n, group(first, n))
            first, count, done = groups_of(sp, NTT - 1)
            with sp.Fori(0, RING) as n:
                load_indices(done + count + n, n)
            sp.wait_ge(S["idx_in"], (done + count) * 16 + 16 * (RING + 1))
            sp.nop(nofuse=True)
            sp.wait_ge(S["d_out0"], 16 * (NB + 1))

        @block.gpsimd
        def _(pool):
            nc.gpsimd.memset(halfneg[:, :], -0.5).then_inc(S["consts"], 1)
            nc.gpsimd.memset(ident[:, :], 0.0).then_inc(S["consts"], 1)
            nc.gpsimd.memset(before[:, :], 1.0).then_inc(S["consts"], 1)
            nc.gpsimd.memset(eps_t[:, :], EPS).then_inc(S["consts"], 1)
            pool.wait_ge(S["consts"], 4)
            nc.gpsimd.affine_select(out=ident[:, :], in_=ident[:, :], compare_op=ALU.not_equal, fill=1.0, base=0,
                                    pattern=[[-1, 128]], channel_multiplier=1).then_inc(S["consts"], 1)
            nc.gpsimd.affine_select(out=before[:, :], in_=before[:, :], compare_op=ALU.is_gt, fill=0.0, base=0,
                                    pattern=[[1, NTT]], channel_multiplier=-1).then_inc(S["consts"], 1)
            for to, step, base in ((iota8, 1, 0), (lane, 1, 0), (tile_neg, -NT, 0), (tile_lo, NT, 0), (group_no, 1, -EG)):
                nc.gpsimd.iota(to[:, :], pattern=[[step, to.shape[1]]], base=base, channel_multiplier=0,
                               allow_small_or_imprecise_dtypes=True).then_inc(S["consts"], 1)
            for b in range(NB):
                pool.wait_ge(S["mv_done"], T * (b + 1))
                nc.gpsimd.tensor_scalar(ve[:, :], mean_var[:, T * b:T * b + T, 1], EPS, None, ALU.add).then_inc(S["pool_ve"], 1)
                pool.wait_ge(S["pool_ve"], b + 1)
                nc.gpsimd.tensor_tensor(rstd[:, T * b:T * b + T], ve[:, :], halfneg[:, :], ALU.pow).then_inc(S["rstd_done"], 1)
            pool.nop().then_inc(S["rows_ready"], RING)
            pool.wait_ge(S["rstd_done"], NB)
            pool.wait_ge(S["ranges"], 1)
            pool.wait_ge(S["x1_out"], 16 * NB)
            _, count, done = groups_of(pool, NTT - 1)
            rounds = (done + count + (RING - 1)) // RING

            def gathers(m):
                for place in range(RING):
                    u = m * RING + place
                    pool.wait_ge(S["idx_in"], u * 16 + 32)
                    pool.wait_ge(S["row_used"], u * EK + EK)
                    pool.nop(nofuse=True)
                    for k in range(EK):
                        at = (place * EK + k) * D
                        pool.indirect_dma_start(RB[:, at:at + D], None, x1_rows,
                                                bass.IndirectOffsetOnAxis(ap=idx[:, place * EK + k:place * EK + k + 1], axis=0)).then_inc(S[f"gath{place}"], 16)
                    if place > 0:
                        pool.wait_ge(S[f"gath{place - 1}"], m * (EK * 16) + EK * 16)
                        pool.nop().then_inc(S["rows_ready"], 1)
                    elif not isinstance(m, int):
                        pool.wait_ge(S[f"gath{RING - 1}"], m * (EK * 16))
                        pool.nop().then_inc(S["rows_ready"], 1)

            gathers(0)
            with pool.Fori(0, rounds - 1) as m:
                gathers(m + 1)
            pool.wait_ge(S[f"gath{RING - 1}"], rounds * (EK * 16))
            pool.nop().then_inc(S["rows_ready"], 1)

        @block.scalar
        def _(act):
            def heads(i):
                act.wait_ge(S["sc_done"], i + 1)
                nc.scalar.activation(probs[:, i % 2, :], shifted_s[:, i % 2, :], ACT.Exp, scale=SCALE).then_inc(S["ex_done"], 1)

            for b in range(NB):
                act.wait_ge(S["tr_done"], b + 1)
                if b >= 2:
                    act.wait_ge(S["proj"], T * (b - 1))
                nc.scalar.copy(xnT[:, b % 2, :, :], pair[b % 2][:, :, 0:QB]).then_inc(S["tr_act"], 1)
                for t in range(T):
                    i = T * b + t
                    act.wait_ge(S["proj"], i + 1)
                    if i >= 2:
                        act.wait_ge(S["x1_done"], i - 1)
                    nc.scalar.copy(qkv[:, i % 2, :], pair[2 + i % 2][0:NT, :, :].rearrange("p a n -> p (a n)")[:, 0:3 * D]).then_inc(S["qkv_done"], 1)
                    if i >= 1:
                        heads(i - 1)
            heads(NTT - 1)

            act.wait_ge(S["d_small"], 16 * 8)
            act.wait_ge(S["dw_prep"], 3)

            def turned(b, n, to):
                act.wait_ge(S["d_hT"], b * 4 + (n + 1))
                nc.scalar.copy(to, pair[3][:, :, 0:QB]).then_inc(S["d_hTe"], 1)

            def deviation(b, n):
                act.wait_ge(S["d_mv"], b * 3 + (n + 1))
                nc.scalar.activation(dsd[:, :], dmv[:, :, 1], ACT.Sqrt, bias=eps_t[:, 0:1]).then_inc(S["d_sd"], 1)

            def ffn(b):
                act.wait_ge(S["d_f1"], b + 1)
                for f in range(FT):
                    nc.scalar.activation(fh[:, f, :], bank[4 + f][:, 0:QB], ACT.Relu, bias=f1b[:, f:f + 1]).then_inc(S["d_fT"], 1)

            def gate_r(b):
                act.wait_ge(S["d_g1"], b + 1)
                for m in range(C):
                    nc.scalar.activation(rT[:, m, :], pair[2][:, m, 0:QB], ACT.Tanh, bias=brz[:, m:m + 1], scale=0.5).then_inc(S["d_tr"], 1)

            def gate_z(b):
                act.wait_ge(S["d_g2"], b + 1)
                for m in range(C):
                    nc.scalar.activation(zT[:, m, :], pair[2][:, m, 0:QB], ACT.Tanh, bias=brz[:, C + m:C + m + 1], scale=0.5).then_inc(S["d_tr"], 1)

            def gate_n(b):
                act.wait_ge(S["d_w"], b + 1)
                for m in range(C):
                    nc.scalar.activation(nT[:, m, :], uT[:, m, :], ACT.Tanh, bias=bih[:, 2 * C + m:2 * C + m + 1]).then_inc(S["d_n"], 1)

            def y_turned(b):
                act.wait_ge(S["d_hT"], b * 4 + 4)
                nc.scalar.copy(hT[:, :, :], pair[3][:, :, 0:QB])
                nc.scalar.copy(yT_of(b), pair[3][:, :, 0:QB]).then_inc(S["d_hTe"], 1)

            def top_exp(b):
                act.wait_ge(S["d_dd"], b + 1)
                nc.scalar.activation(eg[:, :], gap[:, :], ACT.Exp).then_inc(S["d_ex"], 1)

            def comb_turned(b):
                act.wait_ge(S["d_cT"], b + 1)
                nc.scalar.copy(combT[:, :], bank[7][0:NE, 0:QB]).then_inc(S["d_cTe"], 1)

            def relu(b, e):
                for f in range(ET):
                    act.wait_ge(S["d_h1"], b * (NE * ET) + (e * ET + f + 1))
                    if e >= 2 and f == 0:
                        act.wait_ge(S["d_ye"], b * NE + (e - 1))
                    nc.scalar.activation(hid[e % 2][:, f, :], bank[f % 2][:, 0:QB], ACT.Relu, bias=b1s[:, e, f:f + 1]).then_inc(S["d_he"], 1)

            def load_x(b):
                act.wait_ge(S["d_acc0"], b)
                if isinstance(b, int):
                    full = QB if b < NB - 1 else (T - 1) * NT
                    act.dma_start(xd[:, 0:full // NT, :], x[b * QB:b * QB + full, :].rearrange("(t p) d -> p t d", p=NT)).then_inc(S["d_x"], 16)
                    if b == NB - 1:
                        act.dma_start(xd[0:LROWS, T - 1, :], x[b * QB + full:N, :]).then_inc(S["d_x"], 16)
                else:
                    act.dma_start(xd[:, :, :], x[ds(b * QB, QB), :].rearrange("(t p) d -> p t d", p=NT)).then_inc(S["d_x"], 16)

            def load_x1(b):
                act.wait_ge(S["att"], b * 2)
                part = x1_rows[b * QB:(b + 1) * QB, :] if isinstance(b, int) else x1_rows[ds(b * QB, QB), :]
                act.dma_start(x1b[:, :, :], part.rearrange("(t p) d -> p t d", p=NT)).then_inc(S["x1b_in"], 16)

            def store(b):
                act.wait_ge(S["d_acc"], b * NE + NE)
                if isinstance(b, int) and b == NB - 1:
                    full = (T - 1) * NT
                    act.dma_start(out[b * QB:b * QB + full, :].rearrange("(t p) d -> p t d", p=NT), acc_of(b)[:, 0:T - 1, :]).then_inc(S["d_out0"], 16)
                    act.dma_start(out[b * QB + full:N, :], acc_of(b)[0:LROWS, T - 1, :]).then_inc(S["d_out0"], 16)
                else:
                    part = out[b * QB:(b + 1) * QB, :] if isinstance(b, int) else out[ds(b * QB, QB), :]
                    act.dma_start(part.rearrange("(t p) d -> p t d", p=NT), acc_of(b)).then_inc(S["d_out0"], 16)

            def both(x, b, a):
                more = b is not None

                def R(e):
                    if x is not None:
                        relu(x, e)
                R(0)
                if more:
                    turned(b, 0, attT)
                R(1)
                if more:
                    deviation(b, 0)
                R(2)
                if more:
                    turned(b, 1, hT[:, :, :])
                    ffn(b)
                R(3)
                if more:
                    deviation(b, 1)
                R(4)
                if more:
                    turned(b, 2, hT[:, :, :])
                    gate_r(b)
                R(5)
                if more:
                    gate_z(b)
                    gate_n(b)
                R(6)
                if more:
                    deviation(b, 2)
                R(7)
                if more:
                    y_turned(b)
                    top_exp(b)
                    comb_turned(b)
                if x is not None:
                    store(x)
                if more and not (isinstance(b, int) and b == NB - 1):
                    load_x(b + 1)
                if a is not None and not (isinstance(a, int) and a == NB - 1):
                    load_x1(a + 1)

            both(None, None, 0)
            both(None, 0, 1)
            both(0, 1, 2)
            with act.Fori(0, NB - 4) as m:
                both(m + 1, m + 2, m + 3)
            both(NB - 3, NB - 2, NB - 1)
            both(NB - 2, NB - 1, None)
            both(NB - 1, None, None)

        @block.vector
        def _(dve):
            nlink = [0]

            def link(ins):
                nlink[0] += 1
                ins.then_inc(S["chain"], 1)
                dve.wait_ge(S["chain"], nlink[0])

            nc.vector.memset(edge_i[:, 0, :], 0).then_inc(S["pad_set"], 1)
            nc.vector.memset(edge_i[:, 1, :], FAR).then_inc(S["pad_set"], 1)
            nc.vector.memset(x_in[:, NB - 1, T - 1, :], 0.0).then_inc(S["pad_set"], 1)
            nc.vector.memset(zrow[:, :], 0.0).then_inc(S["pad_set"], 1)

            def heads_scores(i):
                r = i % 2
                dve.wait_ge(S["qkv_done"], i + 1)
                q_ = qkv[:, r, 0:D].rearrange("p (h d) -> p h d", h=H).unsqueeze(2).to_broadcast([NT, H, H, DH])
                k_ = qkv[:, r, D:2 * D].rearrange("p (g d) -> p g d", g=H).unsqueeze(1).to_broadcast([NT, H, H, DH])
                link(nc.vector.tensor_tensor(prod.rearrange("p (h g d) -> p h g d", h=H, g=H), q_, k_, ALU.mult))
                link(nc.vector.tensor_reduce(scores, prod.rearrange("p (a d) -> p a d", d=DH), AX, ALU.add))
                link(nc.vector.tensor_reduce(hmax, scores.rearrange("p (h g) -> p h g", h=H), AX, ALU.max))
                nc.vector.tensor_tensor(shifted_s[:, r, :].rearrange("p (h g) -> p h g", h=H), scores.rearrange("p (h g) -> p h g", h=H),
                                        hmax.unsqueeze(2).to_broadcast([NT, H, H]), ALU.subtract).then_inc(S["sc_done"], 1)

            def heads_out(i):
                r = i % 2
                pr = probs[:, r, :].rearrange("p (h g) -> p h g", h=H)
                dve.wait_ge(S["ex_done"], i + 1)
                link(nc.vector.tensor_reduce(hsum, pr, AX, ALU.add))
                link(nc.vector.reciprocal(hinv, hsum))
                link(nc.vector.tensor_tensor(pr, pr, hinv.unsqueeze(2).to_broadcast([NT, H, H]), ALU.mult))
                v_ = qkv[:, r, 2 * D:3 * D].rearrange("p (g d) -> p d g", g=H)
                for h_ in range(H):
                    ins = nc.vector.tensor_tensor(prod.rearrange("p (h d g) -> p h d g", h=H, g=H)[:, h_, :, :], v_,
                                                  pr[:, h_:h_ + 1, :].to_broadcast([NT, DH, H]), ALU.mult)
                link(ins)
                nc.vector.tensor_reduce(x1[:, i, :], prod.rearrange("p (a g) -> p a g", g=H), AX, ALU.add).then_inc(S["x1_done"], 1)
                dve.wait_ge(S["x1_done"], i + 1)

            def ln_block(b):
                r = b % 2
                dve.wait_ge(S[f"x_in{b}"], 32 if b == NB - 1 else 16)
                for t in range(T):
                    nc.vector.bn_stats(stats[:, t, :], x_in[:, b, t, :]).then_inc(S["st_done"], 1)
                dve.wait_ge(S["st_done"], T * (b + 1))
                for t in range(T):
                    nc.vector.bn_aggr(mean_var[:, T * b + t, :], stats[:, t, :]).then_inc(S["mv_done"], 1)
                dve.wait_ge(S["mv_done"], T * (b + 1))
                if b >= 2:
                    dve.wait_ge(S["tr_done"], b - 1)
                dve.wait_ge(S["rstd_done"], b + 1)
                for t in range(T):
                    i = T * b + t
                    nc.vector.tensor_scalar(x_ln[:, r, t, :], x_in[:, b, t, :], mean_var[:, i, 0:1], rstd[:, i:i + 1],
                                            ALU.subtract, ALU.mult).then_inc(S["ln_done"], 1)

            def edge_tables():
                dve.wait_ge(S["edges_in"], 64)
                nc.vector.tensor_copy(edge_f[:, :, :], edge_i[:, :, :]).then_inc(S["edges_f"], 1)
                dve.wait_ge(S["edges_f"], 1)
                nc.vector.tensor_reduce(dmin[:, :], edge_f[:, 1, :], AX, ALU.min)
                link(nc.vector.tensor_reduce(dmax[:, :], edge_f[:, 1, :], AX, ALU.max))
                dve.wait_ge(S["consts"], 11)
                link(nc.vector.tensor_scalar(dmin[:, :], dmin[:, :], float(NT - 1), None, ALU.subtract))
                link(nc.vector.tensor_scalar(not_above[:, :], tile_lo[0:EG, :], dmax[:, 0:1], None, ALU.is_le))
                nc.vector.scalar_tensor_tensor(hit[:, :], tile_lo[0:EG, :], dmin[:, 0:1], not_above[:, :], ALU.is_ge, ALU.mult).then_inc(S["hit_done"], 1)
                dve.wait_ge(S["edges_tr"], 2)
                nc.vector.tensor_copy(src_tab[:, :].rearrange("q (p k) -> q p k", k=EK), bank[6][:, 0:EK * EG].rearrange("q (k p) -> q p k", k=EK)).then_inc(S["tables"], 1)
                nc.vector.tensor_copy(dst_tab[:, :].rearrange("q (p k) -> q p k", k=EK), bank[7][:, 0:EK * EG].rearrange("q (k p) -> q p k", k=EK)).then_inc(S["tables"], 1)
                dve.wait_ge(S["hit_tr"], 1)
                nc.vector.tensor_tensor(cand[:, :], bank[4][0:NTT, 0:EG], group_no[:, :], ALU.mult)
                link(nc.vector.scalar_tensor_tensor(cand_hi[:, :], group_no[:, :], float(EG + 1), bank[4][0:NTT, 0:EG], ALU.add, ALU.mult))
                nc.vector.tensor_reduce(rng[:, 0:1], cand[:, :], AX, ALU.min)
                link(nc.vector.tensor_reduce(rng[:, 1:2], cand_hi[:, :], AX, ALU.max))
                link(nc.vector.tensor_scalar(rng[:, 0:1], rng[:, 0:1], float(EG), float(EG - 1), ALU.add, ALU.min))
                link(nc.vector.scalar_tensor_tensor(rng[:, 1:2], rng[:, 0:1], 1.0, rng[:, 1:2], ALU.add, ALU.max))
                nc.vector.tensor_tensor(rng[:, 2:3], rng[:, 1:2], rng[:, 0:1], ALU.subtract).then_inc(S["rng_done"], 1)
                dve.wait_ge(S["rng_tr"], 1)
                nc.vector.tensor_copy(ranges[:, :], bank[5][0:1, 0:3 * NTT]).then_inc(S["ranges"], 1)

            ln_block(0)
            edge_tables()
            ln_block(1)
            for b in range(NB):
                for t in range(T):
                    heads_scores(T * b + t)
                    if T * b + t >= 1:
                        heads_out(T * b + t - 1)
                if b + 2 < NB:
                    ln_block(b + 2)
            heads_out(NTT - 1)

            dve.wait_ge(S["dw_in"], 16 * 11)
            dve.wait_ge(S["d_small"], 16 * 8)
            nc.vector.tensor_tensor(Wih[:, :, 0:2 * D], Wih[:, :, 0:2 * D], Whh[:, :, 0:2 * D], ALU.add).then_inc(S["dw_prep"], 1)
            nc.vector.tensor_tensor(gb[:, 0, :], gb[:, 0, :], gb[:, 1, :], ALU.add).then_inc(S["dw_prep"], 1)
            link(nc.vector.tensor_tensor(brz[:, :], bih[:, 0:2 * C], bhh[:, 0:2 * C], ALU.add))
            nc.vector.tensor_scalar(brz[:, :], brz[:, :], 0.5, None, ALU.mult).then_inc(S["dw_prep"], 1)
            dve.wait_ge(S["dw_prep"], 3)
            dve.wait_ge(S["tables"], 2)
            dve.wait_ge(S["ranges"], 1)
            d_base = nlink[0]
            D_LINKS = 26

            def edges(i):
                first, count, done = groups_of(dve, i)
                with dve.Fori(0, count) as n:
                    u = done + n
                    for k in range(EK):
                        dve.wait_ge(S["row_used"], u * EK + (CREDIT - EK + k + 1))
                        nc.vector.tensor_scalar(onehot[k][:, :], lane[:, :], dst_tab[:, ds(group(first, n) * EK + k, 1)], col(tile_neg, i),
                                                ALU.subtract, ALU.is_equal).then_inc(S["onehot_set"], 1)

            def attend(b, half_):
                if half_ == 0:
                    dve.wait_ge(S["x1b_in"], b * 16 + 16)
                dve.wait_ge(S["agg"], b * T + (2 * half_ + 2))
                ts = slice(2 * half_, 2 * half_ + 2)
                nc.vector.tensor_tensor(h[:, ts, :], x1b[:, ts, :], by_nodes(2)[:, ts, :], ALU.mult).then_inc(S["att"], 1)

            cnt = [0]

            def dl(b, ins):
                cnt[0] += 1
                ins.then_inc(S["chain"], 1)
                dve.wait_ge(S["chain"], b * D_LINKS + (d_base + cnt[0]))

            def bc(v):
                return vecs[:, v:v + 1, :].to_broadcast([NT, T, D])

            s0 = by_nodes(2)
            s1 = by_nodes(3)

            def ln(b, n, src_, dst_):
                for t in range(T):
                    last = nc.vector.bn_stats(stats[:, t, :], src_[:, t, :])
                dl(b, last)
                dve.nop(nofuse=True)
                for t in range(T):
                    last = nc.vector.bn_aggr(dmv[:, t, :], stats[:, t, :])
                last.then_inc(S["d_mv"], 1)
                dve.wait_ge(S["d_sd"], b * 3 + (n + 1))
                dl(b, nc.vector.reciprocal(drs[:, :], dsd[:, :]))
                for t in range(T):
                    last = nc.vector.tensor_scalar(dst_[:, t, :], src_[:, t, :], dmv[:, t, 0:1], drs[:, t:t + 1], ALU.subtract, ALU.mult)
                return last

            def norm1(b):
                dve.wait_ge(S["d_x"], b * 16 + (32 if isinstance(b, int) and b == NB - 1 else 16))
                dve.wait_ge(S["d_ho"], b + 1)
                mvb = mean_var[:, :, :].rearrange("p i v -> p (i v)")
                for t in range(T):
                    last = nc.vector.tensor_scalar(h[:, t, :], xd[:, t, :], col(mvb, b * (2 * T) + 2 * t), col(rstd, b * T + t), ALU.subtract, ALU.mult)
                dl(b, last)
                dl(b, nc.vector.tensor_tensor(h[:, :, :], h[:, :, :], s0, ALU.add))
                dl(b, nc.vector.tensor_tensor(h[:, :, :], h[:, :, :], bc(0), ALU.add))
                dl(b, ln(b, 0, h, h))
                dl(b, nc.vector.tensor_tensor(h[:, :, :], h[:, :, :], bc(1), ALU.mult))
                nc.vector.tensor_tensor(h[:, :, :], h[:, :, :], bc(2), ALU.add).then_inc(S["d_h"], 1)
                dve.wait_ge(S["d_h"], b * 2 + 1)

            def norm2(b):
                dve.wait_ge(S["d_f2"], b + 1)
                dl(b, nc.vector.tensor_tensor(h[:, :, :], h[:, :, :], s0, ALU.add))
                dl(b, nc.vector.tensor_tensor(h[:, :, :], h[:, :, :], bc(3), ALU.add))
                dl(b, ln(b, 1, h, h))
                dl(b, nc.vector.tensor_tensor(h[:, :, :], h[:, :, :], bc(4), ALU.mult))
                nc.vector.tensor_tensor(h[:, :, :], h[:, :, :], bc(5), ALU.add).then_inc(S["d_h"], 1)

            def gru_r(b):
                dve.wait_ge(S["d_g1"], b + 1)
                for m in range(C):
                    last = nc.vector.tensor_scalar(uT[:, m, :], pair[3][:, m, 0:QB], bhh[:, 2 * C + m:2 * C + m + 1], None, ALU.add)
                last.then_inc(S["d_u"], 1)
                dve.wait_ge(S["d_u"], b + 1)
                dve.wait_ge(S["d_tr"], b * 4 + 2)
                dl(b, nc.vector.scalar_tensor_tensor(uT, rT, 1.0, uT, ALU.add, ALU.mult))

            def gru_out(b):
                dve.wait_ge(S["d_g2"], b + 1)
                nc.vector.scalar_tensor_tensor(uT, uT, 0.5, pair[3][:, :, 0:QB], ALU.mult, ALU.add).then_inc(S["d_w"], 1)
                dve.wait_ge(S["d_n"], b * 2 + 2)
                dl(b, nc.vector.tensor_tensor(uT, hT[:, :, :], nT, ALU.subtract))
                dve.wait_ge(S["d_tr"], b * 4 + 4)
                dl(b, nc.vector.scalar_tensor_tensor(uT, zT, 1.0, uT, ALU.add, ALU.mult))
                nc.vector.scalar_tensor_tensor(uT, uT, 0.5, nT, ALU.mult, ALU.add).then_inc(S["d_gT"], 1)

            def residual(b):
                dve.wait_ge(S["d_gn"], b + 1)
                nc.vector.tensor_tensor(xd[:, :, :], xd[:, :, :], s0, ALU.add).then_inc(S["d_x2"], 1)
                dve.wait_ge(S["d_x2"], b + 1)
                ln(b, 2, xd, h).then_inc(S["d_y"], 1)

            def top2(b):
                dve.wait_ge(S["d_lg"], b + 1)
                dl(b, nc.vector.tensor_tensor(lg[:, :, :], bank[6][0:NT, 0:T * NE].rearrange("p (t e) -> p t e", t=T), gb[:, 0:1, :].to_broadcast([NT, T, NE]), ALU.add))
                dve.nop(nofuse=True)
                for t in range(T):
                    last = nc.vector.max(top[:, t, :], lg[:, t, :])
                dl(b, last)
                dve.nop(nofuse=True)
                for t in range(T):
                    last = nc.vector.max_index(topi[:, t, :], top[:, t, :], lg[:, t, :])
                dl(b, last)
                nc.vector.tensor_tensor(gap[:, :], top[:, :, 1], top[:, :, 0], ALU.subtract).then_inc(S["d_dd"], 1)
                dl(b, nc.vector.tensor_copy(topf[:, :, :], topi[:, :, 0:2]))
                for j in range(2):
                    last = nc.vector.tensor_tensor(oh[:, j, :, :], iota8[:, :].unsqueeze(1).to_broadcast([NT, T, NE]),
                                                   topf[:, :, j:j + 1].to_broadcast([NT, T, NE]), ALU.is_equal)
                dve.wait_ge(S["d_ex"], b + 1)
                dl(b, nc.vector.tensor_scalar(w1[:, :], eg[:, :], 1.0, None, ALU.add))
                dl(b, nc.vector.reciprocal(w1[:, :], w1[:, :]))
                dl(b, nc.vector.tensor_tensor(w2[:, :], eg[:, :], w1[:, :], ALU.mult))
                for j, w in enumerate((w1, w2)):
                    last = nc.vector.tensor_tensor(oh[:, j, :, :], oh[:, j, :, :], w[:, :].unsqueeze(2).to_broadcast([NT, T, NE]), ALU.mult)
                dl(b, last)
                nc.vector.tensor_tensor(comb[:, :, :], oh[:, 0, :, :], oh[:, 1, :, :], ALU.add).then_inc(S["d_comb"], 1)
                nc.vector.tensor_tensor(half(comb_ring, b, T * NE).rearrange("p (t e) -> p t e", t=T), oh[:, 0, :, :], oh[:, 1, :, :], ALU.add).then_inc(S["d_comb"], 1)

            def biases(b):
                dve.wait_ge(S["d_b2"], b + 1)
                if not isinstance(b, int) or b >= 2:
                    dve.wait_ge(S["d_out0"], b * 16 - 16)
                    dve.nop(nofuse=True)
                nc.vector.tensor_tensor(acc_of(b), xd[:, :, :], s1, ALU.add).then_inc(S["d_acc0"], 1)

            def combine(b, e):
                if e == 0:
                    dve.wait_ge(S["d_acc0"], b + 1)
                dve.wait_ge(S["d_ye"], b * NE + (e + 1))
                to = acc_of(b)
                for t in range(T):
                    w = comb_ring[:, (b % 2) * (T * NE) + t * NE + e:(b % 2) * (T * NE) + t * NE + e + 1] if isinstance(b, int) else comb_ring[:, ds((b % 2) * (T * NE) + (t * NE + e), 1)]
                    last = nc.vector.scalar_tensor_tensor(to[:, t, :], by_nodes(1)[:, t, :], w, to[:, t, :], ALU.mult, ALU.add)
                last.then_inc(S["d_acc"], 1)
                dve.wait_ge(S["d_acc"], b * NE + (e + 1))

            def both(x, b, a):
                cnt[0] = 0

                def A(e):
                    if x is not None:
                        combine(x, e)
                if b is not None:
                    norm1(b)
                A(0)
                A(1)
                if b is not None:
                    norm2(b)
                A(2)
                A(3)
                if b is not None:
                    gru_r(b)
                    gru_out(b)
                A(4)
                if b is not None:
                    residual(b)
                A(5)
                A(6)
                if a is not None:
                    edges(a * T)
                if b is not None:
                    top2(b)
                A(7)
                if a is not None:
                    edges(a * T + 1)
                    attend(a, 0)
                    edges(a * T + 2)
                if b is not None:
                    biases(b)
                if a is not None:
                    edges(a * T + 3)
                    attend(a, 1)
                assert b is None or cnt[0] == D_LINKS, cnt[0]

            both(None, None, 0)
            both(None, 0, 1)
            both(0, 1, 2)
            with dve.Fori(0, NB - 3) as m:
                both(m + 1, m + 2, m + 3)
            both(NB - 2, NB - 1, None)
            both(NB - 1, None, None)

        @block.tensor
        def _(pe):
            def edge_tables():
                pe.wait_ge(S["consts"], 5)
                pe.wait_ge(S["edges_f"], 1)
                for w in range(2):
                    for k in range(EK):
                        last = nc.tensor.transpose(bank[6 + w][:, k * EG:(k + 1) * EG], edge_f[:, w, k * 128:(k + 1) * 128], ident[0:EG, 0:EG])
                    last.then_inc(S["edges_tr"], 1)
                pe.wait_ge(S["hit_done"], 1)
                nc.tensor.transpose(bank[4][0:NTT, 0:EG], hit[:, :], ident[0:EG, 0:EG]).then_inc(S["hit_tr"], 1)
                pe.wait_ge(S["rng_done"], 1)
                pe.wait_ge(S["consts"], 11)
                for j, (column, m) in enumerate(((0, ident[0:NTT, 0:NTT]), (2, ident[0:NTT, 0:NTT]), (2, before[:, :]))):
                    last = nc.tensor.matmul(bank[5][0:1, j * NTT:(j + 1) * NTT], rng[:, column:column + 1], m, start=True, stop=True)
                last.then_inc(S["rng_tr"], 1)

            for b in range(NB):
                if b == 0:
                    edge_tables()
                pe.wait_ge(S["ln_done"], T * (b + 1))
                if b >= 2:
                    pe.wait_ge(S["tr_act"], b - 1)
                for c in range(C):
                    for t in range(T):
                        last = nc.tensor.transpose(bank[2 * (b % 2) + c][:, t * NT:(t + 1) * NT], x_ln[:, b % 2, t, c * 128:(c + 1) * 128], ident[0:NT, 0:NT])
                last.then_inc(S["tr_done"], 1)
                pe.wait_ge(S["w_in"], 48)
                pe.wait_ge(S["tables"], 2)
                pe.wait_ge(S["ranges"], 1)
                pe.wait_ge(S["tr_act"], b + 1)
                for t in range(T):
                    i = T * b + t
                    if i >= 2:
                        pe.wait_ge(S["qkv_done"], i - 1)
                    for lo, hi in ((0, SPLIT), (SPLIT, 3 * D)):
                        for c in range(C):
                            last = nc.tensor.matmul(pair[2 + i % 2][0:NT, lo // SPLIT, 0:hi - lo], xnT[:, b % 2, c, t * NT:(t + 1) * NT], wqkv[:, c, lo:hi],
                                                    start=(c == 0), stop=(c == C - 1))
                    last.then_inc(S["proj"], 1)

            pe.nop().then_inc(S["row_used"], CREDIT)
            pe.wait_ge(S["dw_prep"], 3)
            pe.wait_ge(S["qkv_done"], NTT)
            pe.wait_ge(S["pad_set"], 4)

            def edges(i, t):
                first, count, done = groups_of(pe, i)
                to = by_nodes(2)[:, t, :]
                nc.tensor.matmul(to, zrow[:, 0:NT], zrow[:, :], start=True, stop=False)
                with pe.Fori(0, count) as n:
                    u = done + n
                    for k in range(EK):
                        if k == 0:
                            pe.wait_ge(S["rows_ready"], u + (RING + 1))
                        pe.wait_ge(S["onehot_set"], u * EK + (k + 1))
                        nc.tensor.matmul(to, onehot[k][:, :], RB[:, ds((u % RING) * (EK * D) + k * D, D)],
                                         start=False, stop=False).then_inc(S["row_used"], 1)
                nc.tensor.matmul(to, zrow[:, 0:NT], zrow[:, :], start=False, stop=True).then_inc(S["agg"], 1)

            s0 = by_nodes(2)
            s1 = by_nodes(3)

            def by_rows(dst_, lhsT, rhs, steps, done):
                for t in range(T):
                    for c in range(steps):
                        last = nc.tensor.matmul(dst_[:, t, :], lhsT[:, c, t * NT:(t + 1) * NT], rhs[:, c, :], start=(c == 0), stop=(c == steps - 1))
                last.then_inc(S[done], 1)

            def by_features(to, w, lo, rhs):
                for c in range(C):
                    last = nc.tensor.matmul(to[:, 0:QB], w[:, c, lo:lo + 128], rhs[:, c, :], start=(c == 0), stop=(c == C - 1))
                return last

            def turned():
                for c in range(C):
                    for t in range(T):
                        last = nc.tensor.transpose(pair[3][:, c, t * NT:(t + 1) * NT], h[:, t, c * 128:(c + 1) * 128], ident[0:NT, 0:NT])
                last.then_inc(S["d_hT"], 1)

            def att_turned(b):
                pe.wait_ge(S["att"], b * 2 + 2)
                if not (isinstance(b, int) and b == 0):
                    pe.wait_ge(S["d_acc0"], b)
                turned()

            def project(b):
                pe.wait_ge(S["d_hTe"], b * 4 + 1)
                by_rows(s0, attT, Ow, C, "d_ho")

            def h_turned(b, n):
                pe.wait_ge(S["d_h"], b * 2 + n)
                turned()

            def ffn_up(b):
                pe.wait_ge(S["d_hTe"], b * 4 + 2)
                for f in range(FT):
                    last = by_features(bank[4 + f], F1, f * 128, hT)
                last.then_inc(S["d_f1"], 1)

            def ffn_down(b):
                pe.wait_ge(S["d_fT"], b * FT + FT)
                by_rows(s0, fh, F2, FT, "d_f2")

            def gru_r(b):
                pe.wait_ge(S["d_hTe"], b * 4 + 3)
                for m in range(C):
                    by_features(bank[4 + m], Wih, m * 128, hT)
                for m in range(C):
                    last = by_features(bank[6 + m], Whh, (2 * C + m) * 128, hT)
                last.then_inc(S["d_g1"], 1)

            def gru_z(b):
                pe.wait_ge(S["d_tr"], b * 4 + 2)
                for m in range(C):
                    by_features(bank[4 + m], Wih, (C + m) * 128, hT)
                pe.wait_ge(S["d_u"], b + 1)
                for m in range(C):
                    last = by_features(bank[6 + m], Wih, (2 * C + m) * 128, hT)
                last.then_inc(S["d_g2"], 1)

            def gru_turned(b):
                pe.wait_ge(S["d_gT"], b + 1)
                for t in range(T):
                    for c in range(C):
                        last = nc.tensor.transpose(s0[:, t, c * 128:(c + 1) * 128], uT[:, c, t * NT:(t + 1) * NT], ident[:, :])
                last.then_inc(S["d_gn"], 1)

            def y_turned(b):
                pe.wait_ge(S["d_y"], b + 1)
                turned()

            def gate(b):
                pe.wait_ge(S["d_hTe"], b * 4 + 4)
                for t in range(T):
                    for c in range(C):
                        last = nc.tensor.matmul(bank[6][0:NT, t * NE:(t + 1) * NE], hT[:, c, t * NT:(t + 1) * NT], Wgs[:, c, :], start=(c == 0), stop=(c == C - 1))
                last.then_inc(S["d_lg"], 1)

            def comb_turned(b):
                pe.wait_ge(S["d_comb"], b * 2 + 2)
                for t in range(T):
                    last = nc.tensor.transpose(bank[7][0:NE, t * NT:(t + 1) * NT], comb[:, t, :], ident[0:NT, 0:NT])
                last.then_inc(S["d_cT"], 1)

            def out_biases(b):
                pe.wait_ge(S["d_cTe"], b + 1)
                for t in range(T):
                    last = nc.tensor.matmul(s1[:, t, :], combT[:, t * NT:(t + 1) * NT], b2s[:, :], start=True, stop=True)
                last.then_inc(S["d_b2"], 1)

            def up(b, e):
                for f in range(ET):
                    if f >= 2 or e >= 1:
                        pe.wait_ge(S["d_he"], b * (NE * ET) + (e * ET + f - 1))
                    by_features(bank[f % 2], W1s[:, e, :, :], f * 128, yT_of(b)).then_inc(S["d_h1"], 1)

            def down(b, e):
                pe.wait_ge(S["d_he"], b * (NE * ET) + (e + 1) * ET)
                if not (e == 0 and isinstance(b, int) and b == 0):
                    pe.wait_ge(S["d_acc"], b * NE + e)
                by_rows(by_nodes(1), hid[e % 2], W2s[:, e, :, :], ET, "d_ye")

            def both(x, b, a):
                def U(e):
                    if x is not None:
                        up(x, e)

                def D_(e):
                    if x is not None:
                        down(x, e)

                def P(stage, *args):
                    if b is not None:
                        stage(b, *args)

                def G(t):
                    if a is not None:
                        edges(a * T + t, t)

                U(0)
                P(att_turned)
                U(1)
                P(project)
                D_(0)
                U(2)
                P(h_turned, 1)
                D_(1)
                P(ffn_up)
                U(3)
                P(ffn_down)
                D_(2)
                U(4)
                P(h_turned, 2)
                D_(3)
                P(gru_r)
                U(5)
                P(gru_z)
                D_(4)
                U(6)
                P(gru_turned)
                D_(5)
                U(7)
                P(y_turned)
                D_(6)
                P(gate)
                G(0)
                D_(7)
                G(1)
                P(comb_turned)
                G(2)
                P(out_biases)
                G(3)

            both(None, None, 0)
            both(None, 0, 1)
            pe.wait_ge(S["moe_in1"], 16 * NE)
            pe.wait_ge(S["moe_in2"], 16 * NE)
            both(0, 1, 2)
            with pe.Fori(0, NB - 3) as m:
                both(m + 1, m + 2, m + 3)
            both(NB - 2, NB - 1, None)
            both(NB - 1, None, None)


_INS = ['x', 'src', 'dst'] + ['L0_gnn_' + n for n in ('Wq', 'Wk', 'Wv', 'O_w', 'O_b', 'ln1_w', 'ln1_b', 'f1_w', 'f1_b', 'f2_w', 'f2_b',
        'ln2_w', 'ln2_b', 'gru_w_ih', 'gru_w_hh', 'gru_b_ih', 'gru_b_hh')] + ['L0_ffn_' + n for n in ('Wg', 'bg', 'bias', 'W1', 'b1', 'W2', 'b2')]


def kernel(**inputs):
    import numpy as _np
    import concourse.bacc as _bacc
    from concourse import mybir as _mybir
    from concourse.bass_utils import run_bass_kernel_spmd as _run

    nc = _bacc.Bacc("TRN2", target_bir_lowering=False, num_devices=1)
    arrays, args = {}, []
    for name in _INS:
        a = _np.ascontiguousarray(inputs[name])
        arrays[f"in_{name}_dram"] = a
        args.append(nc.dram_tensor(f"in_{name}_dram", a.shape, _mybir.dt.from_np(a.dtype), kind="ExternalInput").ap())
    args.append(nc.dram_tensor("out_0_dram", inputs["x"].shape, _mybir.dt.float32, kind="ExternalOutput").ap())
    gnn_moe_layer(nc, *args)
    r = _run(nc, [arrays], core_ids=[0])
    return r.results[0]["out_0_dram"]
```

```python
import concourse.bass as bass
from concourse import mybir
from contextlib import ExitStack


def gnn_moe_layer(nc, x, src, dst, Wq, Wk, Wv, O_w, O_b, ln1_w, ln1_b, f1_w, f1_b, f2_w, f2_b,
                  ln2_w, ln2_b, w_ih, w_hh, b_ih, b_hh, Wg, bg, gbias, W1, b1, W2, b2, out):
    f32, f16, i32, u32 = mybir.dt.float32, mybir.dt.float16, mybir.dt.int32, mybir.dt.uint32
    ALU, ACT, AX = mybir.AluOpType, mybir.ActivationFunctionType, mybir.AxisListType.X
    ds = bass.ds

    N, D = x.shape
    C = D // 128
    H, DH = 8, 32
    QB = 448
    NB = -(-N // QB)
    NP = NB * QB
    T = 4
    NT = QB // T
    E = src.shape[0]
    EK = 4
    EG = -(-E // (EK * 128))
    ELAST = E - (EG - 1) * EK * 128
    RING = 8
    NTT = NB * T
    FAR = 1000000
    SPLIT = 512
    F = f1_w.shape[1]
    FT = F // 128
    NE, FE = W1.shape[0], W1.shape[2]
    ET = FE // 128
    SCALE = float(DH) ** -0.5
    EPS = 1e-5
    LAST = N - (NB - 1) * QB
    LROWS = LAST - (T - 1) * NT

    x1_rows = nc.dram_tensor("x1_rows", (NP, D), f32, kind="Internal").ap()
    x1_split = nc.dram_tensor("x1_split", (NP, 2 * D), f16, kind="Internal").ap()

    ctx = ExitStack()
    with ctx:
        def sb(name, shape, dt=f32):
            return ctx.enter_context(nc.sbuf_tensor(name, shape, dt))

        def sem(name):
            return ctx.enter_context(nc.semaphore(name))

        QR = 3
        WB = sb("WB", [128, NE * C * FE + NE * ET * D])
        x_in = WB[0:NT, 0:NTT * D].rearrange("p (r t d) -> p r t d", r=NB, t=T)
        o = NTT * D
        x_ln = WB[0:NT, o:o + 2 * T * D].rearrange("p (r t d) -> p r t d", r=2, t=T)
        o += 2 * T * D
        xnT = WB[:, o:o + 2 * C * QB].rearrange("p (r c n) -> p r c n", r=2, c=C)
        o += 2 * C * QB
        qkv = WB[0:NT, o:o + QR * 3 * D].rearrange("p (r w) -> p r w", r=QR)
        o += QR * 3 * D
        prod = WB[0:NT, o:o + H * H * DH]
        o += H * H * DH
        scores = WB[0:NT, o:o + H * H]
        probs = WB[0:NT, o + 64:o + 192].rearrange("p (r w) -> p r w", r=2)
        shifted_s = WB[0:NT, o + 192:o + 320].rearrange("p (r w) -> p r w", r=2)
        hmax, hsum, hinv = (WB[0:NT, o + 320 + 8 * i:o + 328 + 8 * i] for i in range(3))
        o += 344
        cand, cand_hi = (WB[0:NTT, o + i * EG:o + (i + 1) * EG] for i in range(2))
        WU = C * FE
        wsplit = WB[:, :].bitcast(f16).rearrange("p (w l n) -> p w l n", w=2, l=2)
        W1s = [wsplit[:, 0, l, :].rearrange("p (e c f) -> p e c f", e=NE, c=C) for l in range(2)]
        W2s = [wsplit[:, 1, l, :].rearrange("p (e f d) -> p e f d", e=NE, f=ET) for l in range(2)]

        RB = sb("RB", [128, RING * EK * 2 * D], f16)
        x1s = RB[0:NT, 0:NTT * 2 * D].rearrange("p (i w d) -> p i w d", i=NTT, w=2)

        WQKV = sb("WQKV", [128, C * 3 * D])
        wqkv = WQKV[:, :].rearrange("p (c w) -> p c w", c=C)
        vecs = WQKV[0:NT, :].rearrange("p (v d) -> p v d", v=6)

        Ow = sb("Ow", [128, C, D])
        F1 = sb("F1", [128, C, F])
        F2 = sb("F2", [128, FT, D])
        Wih = sb("Wih", [128, C, 3 * D])
        Whh = sb("Whh", [128, C, 3 * D])
        f1b = sb("f1b", [128, FT])
        bih = sb("bih", [128, 3 * C])
        bhh = sb("bhh", [128, 3 * C])
        brz = sb("brz", [128, 2 * C])
        b1s = sb("b1s", [128, NE, ET])
        b2s = sb("b2s", [NE, D])
        Wgs = sb("Wgs", [128, C, NE])
        gb = sb("gb", [NT, 2, NE])

        hT = sb("hT", [128, C, QB])
        yT = [sb(f"yT{l}", [128, 2 * C * QB], f16) for l in range(2)]
        HD = sb("HD", [128, 2 * ET * QB])
        hid16 = HD[:, :].bitcast(f16).rearrange("p (r l f n) -> p r l f n", r=2, l=2, f=ET)
        relu32 = sb("relu32", [128, ET, QB])
        x1 = [HD[0:NT, r * T * D:(r + 1) * T * D].rearrange("p (t d) -> p t d", t=T) for r in range(2)]
        xo = sb("xo", [NT, T, D])
        h = sb("h", [NT, T, D])
        acc = sb("acc", [NT, 2 * T * D])
        xd_x1b = sb("xd_x1b", [NT, 2 * T * D])
        xd = xd_x1b[:, 0:T * D].rearrange("p (t d) -> p t d", t=T)
        x1b = xd_x1b[:, T * D:].rearrange("p (t d) -> p t d", t=T)
        qk = [a[:, :].rearrange("p (h g d) -> p h g d", h=H, g=H) for a in (acc, xd_x1b)]
        gates = sb("gates", [128, 4 * C * QB])
        rT, zT, nT, uT = (gates[:, i * C * QB:(i + 1) * C * QB].rearrange("p (c n) -> p c n", c=C) for i in range(4))
        fh = gates[:, 0:FT * QB].rearrange("p (f n) -> p f n", f=FT)
        attT = nT
        STAGES = 3
        stage = [gates[:, r * WU:(r + 1) * WU] for r in range(STAGES)]
        edge_i = gates[0:EG, 0:2 * EK * 128].bitcast(i32).rearrange("p (w e) -> p w e", w=2)
        edge_f = gates[0:EG, 2 * EK * 128:4 * EK * 128].rearrange("p (w e) -> p w e", w=2)

        ident = sb("ident", [128, 128])
        mean_var = sb("mean_var", [NT, NTT, 2])
        rstd = sb("rstd", [NT, NTT])
        shift = sb("shift", [NT, NTT])
        stats = sb("stats", [NT, T, 6])
        halfneg = sb("halfneg", [NT, T])
        ve = sb("ve", [NT, T])
        eps_t = sb("eps_t", [NT, 1])
        src_tab = sb("src_tab", [128, EG * EK], i32)
        dst_tab = sb("dst_tab", [128, EG * EK])
        idx = sb("idx", [128, RING * EK], i32)
        HR = 6
        onehot = sb("onehot", [128, HR * EK * NT], f16)
        lane = sb("lane", [128, NT], f16)
        tile_neg = sb("tile_neg", [128, NTT])
        tile_lo = sb("tile_lo", [128, NTT])
        group_no = sb("group_no", [NTT, EG])
        dmin = sb("dmin", [EG, 1])
        dmax = sb("dmax", [EG, 1])
        not_above = sb("not_above", [EG, NTT])
        hit = sb("hit", [EG, NTT])
        PACK = 128
        rng = sb("rng", [NTT, 4])
        before = sb("before", [NTT, NTT])
        ranges = sb("ranges", [1, 2 * NTT], i32)
        zrow = sb("zrow", [1, D], f16)
        lg = sb("lg", [NT, T, NE])
        top = sb("top", [NT, T, 8])
        topi = sb("topi", [NT, T, 8], u32)
        topf = sb("topf", [NT, T, 2])
        gap = sb("gap", [NT, T])
        eg = sb("eg", [NT, T])
        w1 = sb("w1", [NT, T])
        w2 = sb("w2", [NT, T])
        oh = sb("oh", [NT, 2, T, NE])
        comb = sb("comb", [NT, T, NE])
        comb_ring = sb("comb_ring", [NT, 2 * T * NE])
        combT = hT[0:NE, 0, :]
        iota8 = sb("iota8", [NT, NE])
        dmv = sb("dmv", [NT, T, 2])
        dsd = sb("dsd", [NT, T])
        drs = sb("drs", [NT, T])

        pair = [ctx.enter_context(nc.psum_tensor(f"pair{i}", [128, 2, 512], f32)) for i in range(4)]
        bank = [pair[i // 2][:, i % 2, :] for i in range(8)]

        def by_nodes(p):
            return pair[p][0:NT, :, :].rearrange("p a (u d) -> p (a u) d", u=2)

        S = {}
        for name in ("w_in x_in0 x_in1 x_in2 x_in3 x_in4 x_in5 x_in6 consts pad_set edges_in edges_f edges_tr tables "
                     "hit_done hit_tr rng_done rng_tr ranges "
                     "st_done mv_done pool_ve pool_rs pool_sh rstd_done ln_done tr_done tr_act proj qkv_done qk_done qk_used sum_done max_done inv_done sc_done ex_done x1_done x1_hi x1_lo x1_stored0 x1_stored1 x1_out chain "
                     "idx_in rows_ready gath0 gath1 gath2 gath3 gath4 gath5 gath6 gath7 onehot_set row_used agg att "
                     "dw_in d_small dw_prep stage_in0 stage_in1 stage_in2 w_hi w_lo "
                     "d_x x1b_in d_hT d_hTe d_ho d_mv d_sd d_h d_f1 d_fT d_f2 d_g1 d_g2 d_tr d_u d_w d_n d_gT d_gn d_x2 d_y d_lg "
                     "d_dd d_ex d_comb d_cT d_cTe d_b2 d_acc0 d_yl d_h1 d_he d_lo d_ye d_acc stored").split():
            S[name] = sem(name)
        WS = 256.0

        block = ctx.enter_context(nc.Block())

        def col(t, c, w=1):
            return t[:, c:c + w] if isinstance(c, int) else t[:, ds(c, w)]

        def half(t, b, size):
            return t[:, (b % 2) * size:(b % 2 + 1) * size] if isinstance(b, int) else t[:, ds((b % 2) * size, size)]

        def acc_of(b):
            return half(acc, b, T * D).rearrange("p (t d) -> p t d", t=T)

        def yT_of(l, b):
            return half(yT[l], b, C * QB).rearrange("p (c n) -> p c n", c=C)

        SUMS = (3, 3, 3, 2)

        def groups_of(eng, i):
            packed = eng.value_load(col(ranges, i), min_val=1, max_val=(EG - 1) * PACK + EG)
            why = "they were packed with these bounds"
            return (nc.s_assert_within(packed // PACK, 0, EG - 1, skip_runtime_bounds_check_because=why),
                    nc.s_assert_within(packed % PACK, 1, EG, skip_runtime_bounds_check_because=why))

        def groups_before(eng, i):
            return eng.value_load(col(ranges, NTT + i), min_val=0, max_val=(NTT - 1) * EG)

        def group(first, n):
            return nc.s_assert_within(first + n, 0, EG - 1, skip_runtime_bounds_check_because="a tile's groups end with the last group")

        @block.sync
        def _(sp):
            for b in range(NB):
                if b < NB - 1:
                    sp.dma_start(x_in[:, b, :, :], x[b * QB:(b + 1) * QB, :].rearrange("(t p) d -> p t d", p=NT)).then_inc(S[f"x_in{b}"], 16)
                else:
                    full = (T - 1) * NT
                    sp.wait_ge(S["pad_set"], 3)
                    sp.dma_start(x_in[:, b, 0:T - 1, :], x[b * QB:b * QB + full, :].rearrange("(t p) d -> p t d", p=NT)).then_inc(S[f"x_in{b}"], 16)
                    sp.dma_start(x_in[0:LROWS, b, T - 1, :], x[b * QB + full:N, :]).then_inc(S[f"x_in{b}"], 16)
                if b == 0:
                    for w, a in enumerate((Wq, Wk, Wv)):
                        sp.dma_start(wqkv[:, :, w * D:(w + 1) * D], a.rearrange("(c p) d -> p c d", p=128)).then_inc(S["w_in"], 16)
                    sp.wait_ge(S["pad_set"], 2)
                    whole = (EG - 1) * EK * 128
                    for w, a in enumerate((src, dst)):
                        sp.dma_start(edge_i[0:EG - 1, w, :], a[0:whole].rearrange("(p e) -> p e", p=EG - 1)).then_inc(S["edges_in"], 16)
                        sp.dma_start(edge_i[EG - 1:EG, w, 0:ELAST], a[whole:E].rearrange("(p e) -> p e", p=1)).then_inc(S["edges_in"], 16)
            with nc.allow_non_contiguous_dma(reason="a few hundred bias words, once"):
                for to, a in ((f1b[:, :], f1_b.rearrange("(f p) -> p f", p=128)), (bih[:, :], b_ih.rearrange("(f p) -> p f", p=128)),
                              (bhh[:, :], b_hh.rearrange("(f p) -> p f", p=128)), (Wgs[:, :, :], Wg.rearrange("(c p) e -> p c e", p=128)),
                              (b2s[:, :], b2), (gb[:, 0, :], bg.partition_broadcast(NT)), (gb[:, 1, :], gbias.partition_broadcast(NT))):
                    sp.dma_start(to, a).then_inc(S["d_small"], 16)
                sp.dma_start(b1s[:, :, :].rearrange("p e f -> p (e f)"), b1.rearrange("e (f p) -> p (e f)", p=128)).then_inc(S["d_small"], 16)
            for to, a in ((Ow, O_w), (F1, f1_w), (F2, f2_w), (Wih, w_ih), (Whh, w_hh)):
                sp.dma_start(to[:, :, :], a.rearrange("(c p) d -> p c d", p=128)).then_inc(S["dw_in"], 16)
            for b in range(NB):
                sp.wait_ge(S["x1_done"], T * (b + 1))
                sp.dma_start(x1_rows[b * QB:(b + 1) * QB, :].rearrange("(t p) d -> p t d", p=NT), x1[b % 2]).then_inc(S[f"x1_stored{b % 2}"], 16)
                sp.wait_ge(S["x1_lo"], T * (b + 1))
                sp.dma_start(x1_split[b * QB:(b + 1) * QB, :].rearrange("(t p) d -> p t d", p=NT), x1s[:, b * T:(b + 1) * T, :, :].rearrange("p t w d -> p t (w d)")).then_inc(S["x1_out"], 16)
            for v, a in enumerate((O_b, ln1_w, ln1_b, f2_b, ln2_w, ln2_b)):
                sp.dma_start(vecs[:, v, :], a.partition_broadcast(NT)).then_inc(S["dw_in"], 16)
            sp.wait_ge(S["x1_stored0"], 16 * (NB - NB // 2))
            sp.wait_ge(S["x1_out"], 16 * NB)

            sp.dma_start(xd[:, :, :], x[0:QB, :].rearrange("(t p) d -> p t d", p=NT)).then_inc(S["d_x"], 16)
            sp.dma_start(x1b[:, :, :], x1_rows[0:QB, :].rearrange("(t p) d -> p t d", p=NT)).then_inc(S["x1b_in"], 16)
            sp.wait_ge(S["tables"], 2)
            sp.wait_ge(S["ranges"], 1)
            sp.nop().then_inc(S["idx_in"], 16)
            def load_indices(u, g):
                sp.wait_ge(S["rows_ready"], u + 1)
                sp.wait_ge(S["idx_in"], u * 16 + 16)
                sp.dma_start(idx[:, ds((u % RING) * EK, EK)], src_tab[:, ds(g * EK, EK)]).then_inc(S["idx_in"], 16)

            with sp.Fori(0, NTT) as i:
                done = groups_before(sp, i)
                first, count = groups_of(sp, i)
                with sp.Fori(0, count) as n:
                    load_indices(done + n, group(first, n))
            done = groups_before(sp, NTT - 1)
            _, count = groups_of(sp, NTT - 1)
            with sp.Fori(0, RING) as n:
                load_indices(done + count + n, n)
            sp.wait_ge(S["idx_in"], (done + count) * 16 + 16 * (RING + 1))
            sp.nop(nofuse=True)
            sp.wait_ge(S["stored"], 16 * (NB + 1))

        @block.gpsimd
        def _(pool):
            nc.gpsimd.memset(halfneg[:, :], -0.5).then_inc(S["consts"], 1)
            nc.gpsimd.memset(ident[:, :], 0.0).then_inc(S["consts"], 1)
            nc.gpsimd.memset(before[:, :], 1.0).then_inc(S["consts"], 1)
            nc.gpsimd.memset(eps_t[:, :], EPS).then_inc(S["consts"], 1)
            pool.wait_ge(S["consts"], 4)
            nc.gpsimd.affine_select(out=ident[:, :], in_=ident[:, :], compare_op=ALU.not_equal, fill=1.0, base=0,
                                    pattern=[[-1, 128]], channel_multiplier=1).then_inc(S["consts"], 1)
            nc.gpsimd.affine_select(out=before[:, :], in_=before[:, :], compare_op=ALU.is_gt, fill=0.0, base=0,
                                    pattern=[[1, NTT]], channel_multiplier=-1).then_inc(S["consts"], 1)
            for to, step, base in ((iota8, 1, 0), (lane, 1, 0), (tile_neg, -NT, 0), (tile_lo, NT, 0), (group_no, 1, -EG)):
                nc.gpsimd.iota(to[:, :], pattern=[[step, to.shape[1]]], base=base, channel_multiplier=0,
                               allow_small_or_imprecise_dtypes=True).then_inc(S["consts"], 1)
            def deviations(b):
                pool.wait_ge(S["mv_done"], T * (b + 1))
                nc.gpsimd.tensor_scalar(ve[:, :], mean_var[:, T * b:T * b + T, 1], EPS, None, ALU.add).then_inc(S["pool_ve"], 1)
                pool.wait_ge(S["pool_ve"], b + 1)
                ts = slice(T * b, T * b + T)
                nc.gpsimd.tensor_tensor(rstd[:, ts], ve[:, :], halfneg[:, :], ALU.pow).then_inc(S["pool_rs"], 1)
                pool.wait_ge(S["pool_rs"], b + 1)
                nc.gpsimd.tensor_tensor(shift[:, ts], mean_var[:, ts, 0], rstd[:, ts], ALU.mult).then_inc(S["pool_sh"], 1)
                pool.wait_ge(S["pool_sh"], b + 1)
                nc.gpsimd.tensor_scalar(shift[:, ts], shift[:, ts], -1.0, None, ALU.mult).then_inc(S["rstd_done"], 1)

            def low_part(i):
                pool.wait_ge(S["x1_hi"], i + 1)
                nc.gpsimd.tensor_tensor(x1s[:, i, 1, :], x1[i // T % 2][:, i % T, :], x1s[:, i, 0, :], ALU.subtract).then_inc(S["x1_lo"], 1)

            deviations(0)
            deviations(1)
            for i in range(NTT):
                r = i % 2
                pool.wait_ge(S["qkv_done"], i + 1)
                if i >= 2:
                    pool.wait_ge(S["qk_used"], i - 1)
                q_ = qkv[:, i % QR, 0:D].rearrange("p (h d) -> p h d", h=H).unsqueeze(2).to_broadcast([NT, H, H, DH])
                k_ = qkv[:, i % QR, D:2 * D].rearrange("p (g d) -> p g d", g=H).unsqueeze(1).to_broadcast([NT, H, H, DH])
                nc.gpsimd.tensor_tensor(qk[r], q_, k_, ALU.mult).then_inc(S["qk_done"], 1)
                if i >= 3:
                    low_part(i - 3)
                if i % T == 0 and i > 0 and i // T + 1 < NB:
                    deviations(i // T + 1)
            for i in range(NTT - 3, NTT):
                low_part(i)
            pool.nop().then_inc(S["rows_ready"], RING)
            pool.wait_ge(S["rstd_done"], NB)
            pool.wait_ge(S["ranges"], 1)
            pool.wait_ge(S["x1_out"], 16 * NB)
            done = groups_before(pool, NTT - 1)
            _, count = groups_of(pool, NTT - 1)
            rounds = (done + count + (RING - 1)) // RING

            def gathers(m):
                for place in range(RING):
                    u = m * RING + place
                    pool.wait_ge(S["idx_in"], u * 16 + 32)
                    pool.wait_ge(S["row_used"], u + 1)
                    pool.nop(nofuse=True)
                    for k in range(EK):
                        at = (place * EK + k) * 2 * D
                        pool.indirect_dma_start(RB[:, at:at + 2 * D], None, x1_split,
                                                bass.IndirectOffsetOnAxis(ap=idx[:, place * EK + k:place * EK + k + 1], axis=0)).then_inc(S[f"gath{place}"], 16)
                    if place > 0:
                        pool.wait_ge(S[f"gath{place - 1}"], m * (EK * 16) + EK * 16)
                        pool.nop().then_inc(S["rows_ready"], 1)
                    elif not isinstance(m, int):
                        pool.wait_ge(S[f"gath{RING - 1}"], m * (EK * 16))
                        pool.nop().then_inc(S["rows_ready"], 1)

            gathers(0)
            with pool.Fori(0, rounds - 1) as m:
                gathers(m + 1)
            pool.wait_ge(S[f"gath{RING - 1}"], rounds * (EK * 16))
            pool.nop().then_inc(S["rows_ready"], 1)

        @block.scalar
        def _(act):
            def high_part(i):
                act.wait_ge(S["x1_done"], i + 1)
                nc.scalar.copy(x1s[:, i, 0, :], x1[i // T % 2][:, i % T, :]).then_inc(S["x1_hi"], 1)

            def heads(i):
                act.wait_ge(S["sc_done"], i + 1)
                nc.scalar.activation(probs[:, i % 2, :], shifted_s[:, i % 2, :], ACT.Exp, scale=SCALE).then_inc(S["ex_done"], 1)

            def normalise(b):
                act.wait_ge(S["rstd_done"], b + 1)
                if b >= 2:
                    act.wait_ge(S["tr_done"], b - 1)
                for t in range(T):
                    i = T * b + t
                    nc.scalar.activation(x_ln[:, b % 2, t, :], x_in[:, b, t, :], ACT.Identity, bias=shift[:, i:i + 1], scale=rstd[:, i:i + 1]).then_inc(S["ln_done"], 1)

            normalise(0)
            normalise(1)
            def features_first(b):
                act.wait_ge(S["tr_done"], b + 1)
                if b >= 2:
                    act.wait_ge(S["proj"], T * (b - 1))
                nc.scalar.copy(xnT[:, b % 2, :, :], pair[b % 2][:, :, 0:QB]).then_inc(S["tr_act"], 1)

            def load_weight(j):
                a = W1[j // 2, :, :] if j % 2 == 0 else W2[j // 2, :, :]
                act.dma_start(stage[j % STAGES].rearrange("p (c f) -> p c f", f=a.shape[1]), a.rearrange("(c p) f -> p c f", p=128)).then_inc(S[f"stage_in{j % STAGES}"], 16)

            features_first(0)
            act.wait_ge(S["edges_tr"], 2)
            for j in range(STAGES):
                load_weight(j)
            for b in range(NB):
                for t in range(T):
                    i = T * b + t
                    act.wait_ge(S["proj"], i + 1)
                    if i >= QR:
                        act.wait_ge(S["x1_done"], i - QR + 1)
                    nc.scalar.copy(qkv[:, i % QR, :], pair[2 + i % 2][0:NT, :, :].rearrange("p a n -> p (a n)")[:, 0:3 * D]).then_inc(S["qkv_done"], 1)
                    if i >= 1:
                        heads(i - 1)
                    if i >= 2:
                        high_part(i - 2)
                    if t == 0 and b >= 1 and b + 1 < NB:
                        normalise(b + 1)
                    if t == 2 and b + 1 < NB:
                        features_first(b + 1)
            high_part(NTT - 2)
            heads(NTT - 1)
            high_part(NTT - 1)

            act.wait_ge(S["x1_lo"], NTT)
            for j in range(2 * NE):
                act.wait_ge(S[f"stage_in{j % STAGES}"], 16 * (j // STAGES + 1))
                nc.scalar.mul(wsplit[:, j % 2, 0, j // 2 * WU:(j // 2 + 1) * WU], stage[j % STAGES], WS).then_inc(S["w_hi"], 1)
                if 1 <= j and j - 1 + STAGES < 2 * NE:
                    act.wait_ge(S["w_lo"], j)
                    load_weight(j - 1 + STAGES)
            act.wait_ge(S["d_small"], 16 * 8)
            act.wait_ge(S["dw_prep"], 3)

            def turned(b, n, to):
                act.wait_ge(S["d_hT"], b * 4 + (n + 1))
                nc.scalar.copy(to, pair[3][:, :, 0:QB]).then_inc(S["d_hTe"], 1)

            def deviation(b, n):
                act.wait_ge(S["d_mv"], b * 3 + (n + 1))
                nc.scalar.activation(dsd[:, :], dmv[:, :, 1], ACT.Sqrt, bias=eps_t[:, 0:1]).then_inc(S["d_sd"], 1)

            def ffn(b):
                act.wait_ge(S["d_f1"], b + 1)
                for f in range(FT):
                    nc.scalar.activation(fh[:, f, :], bank[4 + f][:, 0:QB], ACT.Relu, bias=f1b[:, f:f + 1]).then_inc(S["d_fT"], 1)

            def gate_r(b):
                act.wait_ge(S["d_g1"], b + 1)
                for m in range(C):
                    nc.scalar.activation(rT[:, m, :], pair[2][:, m, 0:QB], ACT.Tanh, bias=brz[:, m:m + 1], scale=0.5).then_inc(S["d_tr"], 1)

            def gate_z(b):
                act.wait_ge(S["d_g2"], b + 1)
                for m in range(C):
                    nc.scalar.activation(zT[:, m, :], pair[2][:, m, 0:QB], ACT.Tanh, bias=brz[:, C + m:C + m + 1], scale=0.5).then_inc(S["d_tr"], 1)

            def gate_n(b):
                act.wait_ge(S["d_w"], b + 1)
                for m in range(C):
                    nc.scalar.activation(nT[:, m, :], uT[:, m, :], ACT.Tanh, bias=bih[:, 2 * C + m:2 * C + m + 1]).then_inc(S["d_n"], 1)

            def y_turned(b):
                act.wait_ge(S["d_hT"], b * 4 + 4)
                nc.scalar.copy(hT[:, :, :], pair[3][:, :, 0:QB])
                nc.scalar.copy(yT_of(0, b), pair[3][:, :, 0:QB]).then_inc(S["d_hTe"], 1)

            def top_exp(b):
                act.wait_ge(S["d_dd"], b + 1)
                nc.scalar.activation(eg[:, :], gap[:, :], ACT.Exp).then_inc(S["d_ex"], 1)

            def comb_turned(b):
                act.wait_ge(S["d_cT"], b + 1)
                nc.scalar.copy(combT, bank[7][0:NE, 0:QB]).then_inc(S["d_cTe"], 1)

            def relu(b, e):
                for f in range(ET):
                    act.wait_ge(S["d_h1"], b * (NE * ET) + (e * ET + f + 1))
                    if e >= 2 and f == 0:
                        act.wait_ge(S["d_ye"], b * NE + (e - 1))
                    if not (isinstance(b, int) and b == 0 and e == 0):
                        act.wait_ge(S["d_lo"], b * (NE * ET) + ((e - 1) * ET + f + 1))
                    nc.scalar.activation(relu32[:, f, :], bank[f % 2][:, 0:QB], ACT.Relu, bias=b1s[:, e, f:f + 1], scale=1.0 / WS)
                    nc.scalar.activation(hid16[:, e % 2, 0, f, :], bank[f % 2][:, 0:QB], ACT.Relu, bias=b1s[:, e, f:f + 1], scale=1.0 / WS).then_inc(S["d_he"], 1)

            def load_x(b):
                act.wait_ge(S["d_acc0"], b)
                if isinstance(b, int):
                    full = QB if b < NB - 1 else (T - 1) * NT
                    act.dma_start(xd[:, 0:full // NT, :], x[b * QB:b * QB + full, :].rearrange("(t p) d -> p t d", p=NT)).then_inc(S["d_x"], 16)
                    if b == NB - 1:
                        act.dma_start(xd[0:LROWS, T - 1, :], x[b * QB + full:N, :]).then_inc(S["d_x"], 16)
                else:
                    act.dma_start(xd[:, :, :], x[ds(b * QB, QB), :].rearrange("(t p) d -> p t d", p=NT)).then_inc(S["d_x"], 16)

            def load_x1(b):
                act.wait_ge(S["d_hT"], b * 4 - 3)
                part = x1_rows[b * QB:(b + 1) * QB, :] if isinstance(b, int) else x1_rows[ds(b * QB, QB), :]
                act.dma_start(x1b[:, :, :], part.rearrange("(t p) d -> p t d", p=NT)).then_inc(S["x1b_in"], 16)

            def store(b):
                act.wait_ge(S["d_acc"], b * NE + NE)
                if isinstance(b, int) and b == NB - 1:
                    full = (T - 1) * NT
                    act.dma_start(out[b * QB:b * QB + full, :].rearrange("(t p) d -> p t d", p=NT), acc_of(b)[:, 0:T - 1, :]).then_inc(S["stored"], 16)
                    act.dma_start(out[b * QB + full:N, :], acc_of(b)[0:LROWS, T - 1, :]).then_inc(S["stored"], 16)
                else:
                    part = out[b * QB:(b + 1) * QB, :] if isinstance(b, int) else out[ds(b * QB, QB), :]
                    act.dma_start(part.rearrange("(t p) d -> p t d", p=NT), acc_of(b)).then_inc(S["stored"], 16)

            def both(x, b, a):
                more = b is not None

                def R(e):
                    if x is not None:
                        relu(x, e)
                R(0)
                if more:
                    turned(b, 0, attT)
                if more and a is not None:
                    load_x1(a)
                R(1)
                if more:
                    deviation(b, 0)
                R(2)
                if more:
                    turned(b, 1, hT[:, :, :])
                    ffn(b)
                R(3)
                if more:
                    deviation(b, 1)
                R(4)
                if more:
                    turned(b, 2, hT[:, :, :])
                    gate_r(b)
                R(5)
                if more:
                    gate_z(b)
                    gate_n(b)
                R(6)
                if more:
                    deviation(b, 2)
                R(7)
                if more:
                    y_turned(b)
                    top_exp(b)
                    comb_turned(b)
                if x is not None:
                    store(x)
                if more and not (isinstance(b, int) and b == NB - 1):
                    load_x(b + 1)

            both(None, None, 0)
            both(None, 0, 1)
            both(0, 1, 2)
            with act.Fori(0, NB - 4) as m:
                both(m + 1, m + 2, m + 3)
            both(NB - 3, NB - 2, NB - 1)
            both(NB - 2, NB - 1, None)
            both(NB - 1, None, None)

        @block.vector
        def _(dve):
            nlink = [0]

            def link(ins):
                nlink[0] += 1
                ins.then_inc(S["chain"], 1)
                dve.wait_ge(S["chain"], nlink[0])

            nc.vector.memset(edge_i[:, 0, :], 0).then_inc(S["pad_set"], 1)
            nc.vector.memset(edge_i[:, 1, :], FAR).then_inc(S["pad_set"], 1)
            nc.vector.memset(x_in[:, NB - 1, T - 1, :], 0.0).then_inc(S["pad_set"], 1)
            nc.vector.memset(zrow[:, :], 0.0).then_inc(S["pad_set"], 1)

            def heads(i):
                scores_, out_ = i < NTT, i >= 1
                r, q = i % 2, (i - 1) % 2
                sc3 = scores.rearrange("p (h g) -> p h g", h=H)
                pr = probs[:, q, :].rearrange("p (h g) -> p h g", h=H)
                if scores_:
                    dve.wait_ge(S["qk_done"], i + 1)
                    if out_:
                        dve.wait_ge(S["sc_done"], i)
                    nc.vector.tensor_reduce(sc3, qk[r], AX, ALU.add).then_inc(S["qk_used"], 1)
                if out_:
                    dve.wait_ge(S["ex_done"], i)
                    nc.vector.tensor_reduce(hsum, pr, AX, ALU.add).then_inc(S["sum_done"], 1)
                if scores_:
                    dve.wait_ge(S["qk_used"], i + 1)
                    nc.vector.tensor_reduce(hmax, sc3, AX, ALU.max).then_inc(S["max_done"], 1)
                if out_:
                    dve.wait_ge(S["sum_done"], i)
                    nc.vector.reciprocal(hinv, hsum).then_inc(S["inv_done"], 1)
                if scores_:
                    dve.wait_ge(S["max_done"], i + 1)
                    nc.vector.tensor_tensor(shifted_s[:, r, :].rearrange("p (h g) -> p h g", h=H), sc3,
                                            hmax.unsqueeze(2).to_broadcast([NT, H, H]), ALU.subtract).then_inc(S["sc_done"], 1)
                if out_:
                    dve.wait_ge(S["inv_done"], i)
                    link(nc.vector.tensor_tensor(pr, pr, hinv.unsqueeze(2).to_broadcast([NT, H, H]), ALU.mult))
                    v_ = qkv[:, (i - 1) % QR, 2 * D:3 * D].rearrange("p (g d) -> p d g", g=H)
                    link(nc.vector.tensor_tensor(prod.rearrange("p (h d g) -> p h d g", h=H, g=H), v_.unsqueeze(1).to_broadcast([NT, H, DH, H]),
                                                 pr.unsqueeze(2).to_broadcast([NT, H, DH, H]), ALU.mult))
                    j = i - 1
                    if j % T == 0 and j >= 2 * T:
                        dve.wait_ge(S[f"x1_stored{j // T % 2}"], 16 * (j // T // 2))
                        dve.wait_ge(S["x1_lo"], j - T)
                    nc.vector.tensor_reduce(x1[j // T % 2][:, j % T, :], prod.rearrange("p (a g) -> p a g", g=H), AX, ALU.add).then_inc(S["x1_done"], 1)
                    dve.wait_ge(S["x1_done"], i)

            def ln_block(b):
                r = b % 2
                dve.wait_ge(S[f"x_in{b}"], 32 if b == NB - 1 else 16)
                for t in range(T):
                    nc.vector.bn_stats(stats[:, t, :], x_in[:, b, t, :]).then_inc(S["st_done"], 1)
                dve.wait_ge(S["st_done"], T * (b + 1))
                for t in range(T):
                    nc.vector.bn_aggr(mean_var[:, T * b + t, :], stats[:, t, :]).then_inc(S["mv_done"], 1)
                dve.wait_ge(S["mv_done"], T * (b + 1))

            def edge_tables():
                dve.wait_ge(S["edges_in"], 64)
                nc.vector.tensor_copy(edge_f[:, :, :], edge_i[:, :, :]).then_inc(S["edges_f"], 1)
                dve.wait_ge(S["edges_f"], 1)
                nc.vector.tensor_reduce(dmin[:, :], edge_f[:, 1, :], AX, ALU.min)
                link(nc.vector.tensor_reduce(dmax[:, :], edge_f[:, 1, :], AX, ALU.max))
                dve.wait_ge(S["consts"], 11)
                link(nc.vector.tensor_scalar(dmin[:, :], dmin[:, :], float(NT - 1), None, ALU.subtract))
                link(nc.vector.tensor_scalar(not_above[:, :], tile_lo[0:EG, :], dmax[:, 0:1], None, ALU.is_le))
                nc.vector.scalar_tensor_tensor(hit[:, :], tile_lo[0:EG, :], dmin[:, 0:1], not_above[:, :], ALU.is_ge, ALU.mult).then_inc(S["hit_done"], 1)
                dve.wait_ge(S["edges_tr"], 2)
                nc.vector.tensor_copy(src_tab[:, :].rearrange("q (p k) -> q p k", k=EK), bank[6][:, 0:EK * EG].rearrange("q (k p) -> q p k", k=EK)).then_inc(S["tables"], 1)
                nc.vector.tensor_copy(dst_tab[:, :].rearrange("q (p k) -> q p k", k=EK), bank[7][:, 0:EK * EG].rearrange("q (k p) -> q p k", k=EK)).then_inc(S["tables"], 1)
                dve.wait_ge(S["hit_tr"], 1)
                nc.vector.tensor_tensor(cand, bank[4][0:NTT, 0:EG], group_no[:, :], ALU.mult)
                link(nc.vector.scalar_tensor_tensor(cand_hi, group_no[:, :], float(EG + 1), bank[4][0:NTT, 0:EG], ALU.add, ALU.mult))
                nc.vector.tensor_reduce(rng[:, 0:1], cand, AX, ALU.min)
                link(nc.vector.tensor_reduce(rng[:, 1:2], cand_hi, AX, ALU.max))
                link(nc.vector.tensor_scalar(rng[:, 0:1], rng[:, 0:1], float(EG), float(EG - 1), ALU.add, ALU.min))
                link(nc.vector.scalar_tensor_tensor(rng[:, 1:2], rng[:, 0:1], 1.0, rng[:, 1:2], ALU.add, ALU.max))
                link(nc.vector.tensor_tensor(rng[:, 2:3], rng[:, 1:2], rng[:, 0:1], ALU.subtract))
                nc.vector.scalar_tensor_tensor(rng[:, 3:4], rng[:, 0:1], float(PACK), rng[:, 2:3], ALU.mult, ALU.add).then_inc(S["rng_done"], 1)
                dve.wait_ge(S["rng_tr"], 1)
                nc.vector.tensor_copy(ranges[:, :], bank[5][0:1, 0:2 * NTT]).then_inc(S["ranges"], 1)

            ln_block(0)
            edge_tables()
            ln_block(1)
            for b in range(NB):
                for t in range(T):
                    heads(T * b + t)
                if b + 2 < NB:
                    ln_block(b + 2)
            heads(NTT)

            def weights_low(lo, hi):
                for j in range(lo, hi):
                    dve.wait_ge(S["w_hi"], j + 1)
                    part = wsplit[:, j % 2, :, j // 2 * WU:(j // 2 + 1) * WU]
                    nc.vector.scalar_tensor_tensor(part[:, 1, :], stage[j % STAGES], WS, part[:, 0, :], ALU.mult, ALU.subtract).then_inc(S["w_lo"], 1)

            dve.wait_ge(S["dw_in"], 16 * 11)
            dve.wait_ge(S["d_small"], 16 * 8)
            nc.vector.tensor_tensor(Wih[:, :, 0:2 * D], Wih[:, :, 0:2 * D], Whh[:, :, 0:2 * D], ALU.add).then_inc(S["dw_prep"], 1)
            nc.vector.tensor_tensor(gb[:, 0, :], gb[:, 0, :], gb[:, 1, :], ALU.add).then_inc(S["dw_prep"], 1)
            link(nc.vector.tensor_tensor(brz[:, :], bih[:, 0:2 * C], bhh[:, 0:2 * C], ALU.add))
            nc.vector.tensor_scalar(brz[:, :], brz[:, :], 0.5, None, ALU.mult).then_inc(S["dw_prep"], 1)
            dve.wait_ge(S["dw_prep"], 3)
            dve.wait_ge(S["tables"], 2)
            dve.wait_ge(S["ranges"], 1)
            d_base = nlink[0]
            D_LINKS = 22

            def edges(i, done, groups):
                first, count = groups
                dve.nop(nofuse=True)
                with dve.Fori(0, count) as n:
                    u = done + n
                    ones = onehot[:, ds((u % HR) * (EK * NT), EK * NT)]
                    ends = dst_tab[:, ds(group(first, n) * EK, EK)]
                    dve.wait_ge(S["row_used"], u + (RING - HR + 1))
                    for k in range(EK):
                        last = nc.vector.tensor_scalar(ones[:, k * NT:(k + 1) * NT], lane[:, :], ends[:, k:k + 1], col(tile_neg, i),
                                                       ALU.subtract, ALU.is_equal)
                    last.then_inc(S["onehot_set"], 1)
                return done + count

            def attend(b, t):
                if t == 0:
                    dve.wait_ge(S["x1b_in"], b * 16 + 16)
                dve.wait_ge(S["agg"], b * T + (t + 1))
                nc.vector.tensor_tensor(x1b[:, t, :], x1b[:, t, :], by_nodes(SUMS[t])[:, 0, :], ALU.mult).then_inc(S["att"], 1)

            cnt = [0]

            def dl(b, ins):
                cnt[0] += 1
                ins.then_inc(S["chain"], 1)
                dve.wait_ge(S["chain"], b * D_LINKS + (d_base + cnt[0]))

            def bc(v):
                return vecs[:, v:v + 1, :].to_broadcast([NT, T, D])

            s0 = by_nodes(2)
            s1 = by_nodes(3)

            def moments(b, n, src_):
                for t in range(T):
                    last = nc.vector.bn_stats(stats[:, t, :], src_[:, t, :])
                dl(b, last)
                dve.nop(nofuse=True)
                for t in range(T):
                    last = nc.vector.bn_aggr(dmv[:, t, :], stats[:, t, :])
                last.then_inc(S["d_mv"], 1)
                dve.wait_ge(S["d_mv"], b * 3 + (n + 1))

            def weighted_norm(b, n, w):
                moments(b, n, h)
                for t in range(T):
                    last = nc.vector.scalar_tensor_tensor(h[:, t, :], h[:, t, :], dmv[:, t, 0:1], vecs[:, w, :], ALU.subtract, ALU.mult)
                dve.wait_ge(S["d_sd"], b * 3 + (n + 1))
                dl(b, nc.vector.reciprocal(drs[:, :], dsd[:, :]))
                for t in range(T):
                    last = nc.vector.scalar_tensor_tensor(h[:, t, :], h[:, t, :], drs[:, t:t + 1], vecs[:, w + 1, :], ALU.mult, ALU.add)
                last.then_inc(S["d_h"], 1)
                dve.wait_ge(S["d_h"], b * 2 + (n + 1))

            def norm_x(b):
                dve.wait_ge(S["d_x"], b * 16 + (32 if isinstance(b, int) and b == NB - 1 else 16))
                mvb = mean_var[:, :, :].rearrange("p i v -> p (i v)")
                for t in range(T):
                    last = nc.vector.tensor_scalar(xo[:, t, :], xd[:, t, :], col(mvb, b * (2 * T) + 2 * t), col(rstd, b * T + t), ALU.subtract, ALU.mult)
                dl(b, last)
                dl(b, nc.vector.tensor_tensor(xo[:, :, :], xo[:, :, :], bc(0), ALU.add))

            def norm1(b):
                dve.wait_ge(S["d_ho"], b + 1)
                dl(b, nc.vector.tensor_tensor(h[:, :, :], xo[:, :, :], s0, ALU.add))
                weighted_norm(b, 0, 1)

            def add_bias2(b):
                dve.wait_ge(S["d_hT"], b * 4 + 2)
                dl(b, nc.vector.tensor_tensor(h[:, :, :], h[:, :, :], bc(3), ALU.add))

            def norm2(b):
                dve.wait_ge(S["d_f2"], b + 1)
                dl(b, nc.vector.tensor_tensor(h[:, :, :], h[:, :, :], s0, ALU.add))
                weighted_norm(b, 1, 4)

            def gru_r(b):
                dve.wait_ge(S["d_g1"], b + 1)
                for m in range(C):
                    last = nc.vector.tensor_scalar(uT[:, m, :], pair[3][:, m, 0:QB], bhh[:, 2 * C + m:2 * C + m + 1], None, ALU.add)
                last.then_inc(S["d_u"], 1)
                dve.wait_ge(S["d_u"], b + 1)
                dve.wait_ge(S["d_tr"], b * 4 + 2)
                dl(b, nc.vector.scalar_tensor_tensor(uT, rT, 1.0, uT, ALU.add, ALU.mult))

            def gru_out(b):
                dve.wait_ge(S["d_g2"], b + 1)
                nc.vector.scalar_tensor_tensor(uT, uT, 0.5, pair[3][:, :, 0:QB], ALU.mult, ALU.add).then_inc(S["d_w"], 1)
                dve.wait_ge(S["d_n"], b * 2 + 2)
                dl(b, nc.vector.tensor_tensor(uT, hT[:, :, :], nT, ALU.subtract))
                dve.wait_ge(S["d_tr"], b * 4 + 4)
                dl(b, nc.vector.scalar_tensor_tensor(uT, zT, 1.0, uT, ALU.add, ALU.mult))
                nc.vector.scalar_tensor_tensor(uT, uT, 0.5, nT, ALU.mult, ALU.add).then_inc(S["d_gT"], 1)

            def residual(b):
                dve.wait_ge(S["d_gn"], b + 1)
                nc.vector.tensor_tensor(xd[:, :, :], xd[:, :, :], s0, ALU.add).then_inc(S["d_x2"], 1)
                dve.wait_ge(S["d_x2"], b + 1)
                moments(b, 2, xd)
                dve.wait_ge(S["d_sd"], b * 3 + 3)
                dl(b, nc.vector.reciprocal(drs[:, :], dsd[:, :]))
                for t in range(T):
                    last = nc.vector.tensor_scalar(h[:, t, :], xd[:, t, :], dmv[:, t, 0:1], drs[:, t:t + 1], ALU.subtract, ALU.mult)
                last.then_inc(S["d_y"], 1)

            def top2(b):
                dve.wait_ge(S["d_lg"], b + 1)
                dl(b, nc.vector.tensor_tensor(lg[:, :, :], bank[6][0:NT, 0:T * NE].rearrange("p (t e) -> p t e", t=T), gb[:, 0:1, :].to_broadcast([NT, T, NE]), ALU.add))
                dve.nop(nofuse=True)
                for t in range(T):
                    last = nc.vector.max(top[:, t, :], lg[:, t, :])
                dl(b, last)
                dve.nop(nofuse=True)
                for t in range(T):
                    last = nc.vector.max_index(topi[:, t, :], top[:, t, :], lg[:, t, :])
                dl(b, last)
                nc.vector.tensor_tensor(gap[:, :], top[:, :, 1], top[:, :, 0], ALU.subtract).then_inc(S["d_dd"], 1)
                dl(b, nc.vector.tensor_copy(topf[:, :, :], topi[:, :, 0:2]))
                for j in range(2):
                    last = nc.vector.tensor_tensor(oh[:, j, :, :], iota8[:, :].unsqueeze(1).to_broadcast([NT, T, NE]),
                                                   topf[:, :, j:j + 1].to_broadcast([NT, T, NE]), ALU.is_equal)
                dve.wait_ge(S["d_ex"], b + 1)
                dl(b, nc.vector.tensor_scalar(w1[:, :], eg[:, :], 1.0, None, ALU.add))
                dl(b, nc.vector.reciprocal(w1[:, :], w1[:, :]))
                dl(b, nc.vector.tensor_tensor(w2[:, :], eg[:, :], w1[:, :], ALU.mult))
                for j, w in enumerate((w1, w2)):
                    last = nc.vector.tensor_tensor(oh[:, j, :, :], oh[:, j, :, :], w[:, :].unsqueeze(2).to_broadcast([NT, T, NE]), ALU.mult)
                dl(b, last)
                nc.vector.tensor_tensor(comb[:, :, :], oh[:, 0, :, :], oh[:, 1, :, :], ALU.add).then_inc(S["d_comb"], 1)
                dve.wait_ge(S["d_comb"], b * 2 + 1)
                nc.vector.tensor_scalar(half(comb_ring, b, T * NE).rearrange("p (t e) -> p t e", t=T), comb[:, :, :], 1.0 / WS, None, ALU.mult).then_inc(S["d_comb"], 1)

            def y_low(b):
                dve.wait_ge(S["d_hTe"], b * 4 + 4)
                nc.vector.tensor_tensor(yT_of(1, b), pair[3][:, :, 0:QB], yT_of(0, b), ALU.subtract).then_inc(S["d_yl"], 1)

            def hidden_low(b, e):
                for f in range(ET):
                    dve.wait_ge(S["d_he"], b * (NE * ET) + (e * ET + f + 1))
                    nc.vector.tensor_tensor(hid16[:, e % 2, 1, f, :], relu32[:, f, :], hid16[:, e % 2, 0, f, :], ALU.subtract).then_inc(S["d_lo"], 1)

            def biases(b):
                dve.wait_ge(S["d_b2"], b + 1)
                if not isinstance(b, int) or b >= 2:
                    dve.wait_ge(S["stored"], b * 16 - 16)
                    dve.nop(nofuse=True)
                nc.vector.tensor_tensor(acc_of(b), xd[:, :, :], s1, ALU.add).then_inc(S["d_acc0"], 1)

            def combine(b, e):
                if e == 0:
                    dve.wait_ge(S["d_acc0"], b + 1)
                dve.wait_ge(S["d_ye"], b * NE + (e + 1))
                to = acc_of(b)
                for t in range(T):
                    w = comb_ring[:, (b % 2) * (T * NE) + t * NE + e:(b % 2) * (T * NE) + t * NE + e + 1] if isinstance(b, int) else comb_ring[:, ds((b % 2) * (T * NE) + (t * NE + e), 1)]
                    last = nc.vector.scalar_tensor_tensor(to[:, t, :], by_nodes(1)[:, t, :], w, to[:, t, :], ALU.mult, ALU.add)
                last.then_inc(S["d_acc"], 1)
                dve.wait_ge(S["d_acc"], b * NE + (e + 1))

            def both(x, b, a):
                cnt[0] = 0

                def A(e):
                    if x is not None:
                        combine(x, e)
                def L(e):
                    if x is not None:
                        hidden_low(x, e)

                def P(stage_):
                    if b is not None:
                        stage_(b)

                def F(t):
                    if a is None:
                        return None
                    dve.nop(nofuse=True)
                    return groups_of(dve, a * T + t)

                def G(t, done, groups):
                    return None if a is None else edges(a * T + t, done, groups)

                def M(t):
                    if a is not None:
                        attend(a, t)

                dve.nop(nofuse=True)
                done = None if a is None else groups_before(dve, a * T)
                groups = F(0)
                L(0)
                P(norm_x)
                done = G(0, done, groups)
                L(1)
                P(norm1)
                M(0)
                A(0)
                L(2)
                P(add_bias2)
                groups = F(1)
                A(1)
                done = G(1, done, groups)
                L(3)
                P(norm2)
                M(1)
                A(2)
                L(4)
                A(3)
                P(gru_r)
                L(5)
                P(gru_out)
                groups = F(2)
                A(4)
                done = G(2, done, groups)
                L(6)
                P(residual)
                M(2)
                A(5)
                L(7)
                P(y_low)
                groups = F(3)
                G(3, done, groups)
                A(6)
                P(top2)
                M(3)
                A(7)
                P(biases)
                assert b is None or cnt[0] == D_LINKS, cnt[0]

            done = groups_before(dve, 0)
            for t in range(T):
                weights_low(t * 2 * NE // T, (t + 1) * 2 * NE // T)
                dve.nop(nofuse=True)
                done = edges(t, done, groups_of(dve, t))
                attend(0, t)
            both(None, 0, 1)
            both(0, 1, 2)
            with dve.Fori(0, NB - 3) as m:
                both(m + 1, m + 2, m + 3)
            both(NB - 2, NB - 1, None)
            both(NB - 1, None, None)

        @block.tensor
        def _(pe):
            def edge_tables():
                pe.wait_ge(S["consts"], 5)
                pe.wait_ge(S["edges_f"], 1)
                for w in range(2):
                    for k in range(EK):
                        last = nc.tensor.transpose(bank[6 + w][:, k * EG:(k + 1) * EG], edge_f[:, w, k * 128:(k + 1) * 128], ident[0:EG, 0:EG])
                    last.then_inc(S["edges_tr"], 1)
                pe.wait_ge(S["hit_done"], 1)
                nc.tensor.transpose(bank[4][0:NTT, 0:EG], hit[:, :], ident[0:EG, 0:EG]).then_inc(S["hit_tr"], 1)
                pe.wait_ge(S["rng_done"], 1)
                pe.wait_ge(S["consts"], 11)
                for j, (column, m) in enumerate(((3, ident[0:NTT, 0:NTT]), (2, before[:, :]))):
                    last = nc.tensor.matmul(bank[5][0:1, j * NTT:(j + 1) * NTT], rng[:, column:column + 1], m, start=True, stop=True)
                last.then_inc(S["rng_tr"], 1)

            def features_first(b):
                pe.wait_ge(S["ln_done"], T * (b + 1))
                if b >= 2:
                    pe.wait_ge(S["tr_act"], b - 1)
                for c in range(C):
                    for t in range(T):
                        last = nc.tensor.transpose(bank[2 * (b % 2) + c][:, t * NT:(t + 1) * NT], x_ln[:, b % 2, t, c * 128:(c + 1) * 128], ident[0:NT, 0:NT])
                last.then_inc(S["tr_done"], 1)

            edge_tables()
            features_first(0)
            pe.wait_ge(S["w_in"], 48)
            pe.wait_ge(S["tables"], 2)
            pe.wait_ge(S["ranges"], 1)
            for i in range(NTT):
                b, t = i // T, i % T
                if t == 0:
                    pe.wait_ge(S["tr_act"], b + 1)
                if i >= 2:
                    pe.wait_ge(S["qkv_done"], i - 1)
                for lo, hi in ((0, SPLIT), (SPLIT, 3 * D)):
                    for c in range(C):
                        last = nc.tensor.matmul(pair[2 + i % 2][0:NT, lo // SPLIT, 0:hi - lo], xnT[:, b % 2, c, t * NT:(t + 1) * NT], wqkv[:, c, lo:hi],
                                                start=(c == 0), stop=(c == C - 1))
                last.then_inc(S["proj"], 1)
                if t == 1 and b + 1 < NB:
                    features_first(b + 1)

            pe.nop().then_inc(S["row_used"], RING)
            pe.wait_ge(S["dw_prep"], 3)
            pe.wait_ge(S["qkv_done"], NTT)
            pe.wait_ge(S["pad_set"], 4)

            def edges(i, t, done, count):
                to = by_nodes(SUMS[t])[:, 0, :]
                if not (isinstance(i, int) and i == 0):
                    pe.wait_ge(S["att"], i)
                nc.tensor.matmul(to, zrow[:, 0:NT], zrow[:, :], start=True, stop=False)
                with pe.Fori(0, count) as n:
                    u = done + n
                    rows = RB[:, ds((u % RING) * (EK * 2 * D), EK * 2 * D)]
                    ones = onehot[:, ds((u % HR) * (EK * NT), EK * NT)]
                    pe.wait_ge(S["rows_ready"], u + (RING + 1))
                    pe.wait_ge(S["onehot_set"], u + 1)
                    for k in range(EK):
                        for w in range(2):
                            at = (2 * k + w) * D
                            last = nc.tensor.matmul(to, ones[:, k * NT:(k + 1) * NT], rows[:, at:at + D], start=False, stop=False)
                    last.then_inc(S["row_used"], 1)
                nc.tensor.matmul(to, zrow[:, 0:NT], zrow[:, :], start=False, stop=True).then_inc(S["agg"], 1)
                return done + count

            s0 = by_nodes(2)
            s1 = by_nodes(3)

            def by_rows(dst_, lhsT, rhs, steps, done):
                for t in range(T):
                    for c in range(steps):
                        last = nc.tensor.matmul(dst_[:, t, :], lhsT[:, c, t * NT:(t + 1) * NT], rhs[:, c, :], start=(c == 0), stop=(c == steps - 1))
                last.then_inc(S[done], 1)

            def by_features(to, w, lo, rhs):
                for c in range(C):
                    last = nc.tensor.matmul(to[:, 0:QB], w[:, c, lo:lo + 128], rhs[:, c, :], start=(c == 0), stop=(c == C - 1))
                return last

            def turned(rows_):
                for c in range(C):
                    for t in range(T):
                        last = nc.tensor.transpose(pair[3][:, c, t * NT:(t + 1) * NT], rows_[:, t, c * 128:(c + 1) * 128], ident[0:NT, 0:NT])
                last.then_inc(S["d_hT"], 1)

            def att_turned(b):
                pe.wait_ge(S["att"], b * T + T)
                if not (isinstance(b, int) and b == 0):
                    pe.wait_ge(S["d_acc0"], b)
                turned(x1b)

            def project(b):
                pe.wait_ge(S["d_hTe"], b * 4 + 1)
                by_rows(s0, attT, Ow, C, "d_ho")

            def h_turned(b, n):
                pe.wait_ge(S["d_h"], b * 2 + n)
                turned(h)

            def ffn_up(b):
                pe.wait_ge(S["d_hTe"], b * 4 + 2)
                for f in range(FT):
                    last = by_features(bank[4 + f], F1, f * 128, hT)
                last.then_inc(S["d_f1"], 1)

            def ffn_down(b):
                pe.wait_ge(S["d_fT"], b * FT + FT)
                by_rows(s0, fh, F2, FT, "d_f2")

            def gru_r(b):
                pe.wait_ge(S["d_hTe"], b * 4 + 3)
                for m in range(C):
                    by_features(bank[4 + m], Wih, m * 128, hT)
                for m in range(C):
                    last = by_features(bank[6 + m], Whh, (2 * C + m) * 128, hT)
                last.then_inc(S["d_g1"], 1)

            def gru_z(b):
                pe.wait_ge(S["d_tr"], b * 4 + 2)
                for m in range(C):
                    by_features(bank[4 + m], Wih, (C + m) * 128, hT)
                pe.wait_ge(S["d_u"], b + 1)
                for m in range(C):
                    last = by_features(bank[6 + m], Wih, (2 * C + m) * 128, hT)
                last.then_inc(S["d_g2"], 1)

            def gru_turned(b):
                pe.wait_ge(S["d_gT"], b + 1)
                for t in range(T):
                    for c in range(C):
                        last = nc.tensor.transpose(s0[:, t, c * 128:(c + 1) * 128], uT[:, c, t * NT:(t + 1) * NT], ident[:, :])
                last.then_inc(S["d_gn"], 1)

            def y_turned(b):
                pe.wait_ge(S["d_y"], b + 1)
                turned(h)

            def gate(b):
                pe.wait_ge(S["d_hTe"], b * 4 + 4)
                pe.wait_ge(S["d_yl"], b + 1)
                for t in range(T):
                    for c in range(C):
                        last = nc.tensor.matmul(bank[6][0:NT, t * NE:(t + 1) * NE], hT[:, c, t * NT:(t + 1) * NT], Wgs[:, c, :], start=(c == 0), stop=(c == C - 1))
                last.then_inc(S["d_lg"], 1)

            def comb_turned(b):
                pe.wait_ge(S["d_comb"], b * 2 + 2)
                for t in range(T):
                    last = nc.tensor.transpose(bank[7][0:NE, t * NT:(t + 1) * NT], comb[:, t, :], ident[0:NT, 0:NT])
                last.then_inc(S["d_cT"], 1)

            def out_biases(b):
                pe.wait_ge(S["d_cTe"], b + 1)
                for t in range(T):
                    last = nc.tensor.matmul(s1[:, t, :], combT[:, t * NT:(t + 1) * NT], b2s[:, :], start=True, stop=True)
                last.then_inc(S["d_b2"], 1)

            PARTS = ((0, 0), (0, 1), (1, 0))

            def up(b, e):
                for f in range(ET):
                    if f >= 2 or e >= 1:
                        pe.wait_ge(S["d_he"], b * (NE * ET) + (e * ET + f - 1))
                    for n, (wl, yl) in enumerate(PARTS):
                        for c in range(C):
                            last = nc.tensor.matmul(bank[f % 2][:, 0:QB], W1s[wl][:, e, c, f * 128:(f + 1) * 128], yT_of(yl, b)[:, c, :],
                                                    start=(n == 0 and c == 0), stop=(n == len(PARTS) - 1 and c == C - 1))
                    last.then_inc(S["d_h1"], 1)

            def down(b, e):
                pe.wait_ge(S["d_lo"], b * (NE * ET) + (e + 1) * ET)
                if not (e == 0 and isinstance(b, int) and b == 0):
                    pe.wait_ge(S["d_acc"], b * NE + e)
                for t in range(T):
                    for n, (hl, wl) in enumerate(PARTS):
                        for f in range(ET):
                            last = nc.tensor.matmul(by_nodes(1)[:, t, :], hid16[:, e % 2, hl, f, t * NT:(t + 1) * NT], W2s[wl][:, e, f, :],
                                                    start=(n == 0 and f == 0), stop=(n == len(PARTS) - 1 and f == ET - 1))
                last.then_inc(S["d_ye"], 1)

            def both(x, b, a):
                def U(e):
                    if x is not None:
                        up(x, e)

                def D_(e):
                    if x is not None:
                        down(x, e)

                def P(stage, *args):
                    if b is not None:
                        stage(b, *args)

                def F(t):
                    if a is None:
                        return None
                    pe.nop(nofuse=True)
                    return groups_of(pe, a * T + t)[1]

                def G(t, done, count):
                    return None if a is None else edges(a * T + t, t, done, count)

                def freed(t):
                    if a is not None:
                        pe.wait_ge(S["att"], a * T + (t + 1))

                U(0)
                P(att_turned)
                U(1)
                pe.nop(nofuse=True)
                done = None if a is None else groups_before(pe, a * T)
                count = F(0)
                P(project)
                done = G(0, done, count)
                D_(0)
                U(2)
                freed(0)
                P(h_turned, 1)
                D_(1)
                P(ffn_up)
                U(3)
                count = F(1)
                P(ffn_down)
                done = G(1, done, count)
                D_(2)
                U(4)
                freed(1)
                P(h_turned, 2)
                D_(3)
                P(gru_r)
                U(5)
                P(gru_z)
                D_(4)
                U(6)
                count = F(2)
                P(gru_turned)
                done = G(2, done, count)
                D_(5)
                U(7)
                freed(2)
                P(y_turned)
                count = F(3)
                D_(6)
                P(gate)
                G(3, done, count)
                D_(7)
                P(comb_turned)
                P(out_biases)

            both(None, None, 0)
            both(None, 0, 1)
            pe.wait_ge(S["w_lo"], 2 * NE)
            both(0, 1, 2)
            with pe.Fori(0, NB - 3) as m:
                both(m + 1, m + 2, m + 3)
            both(NB - 2, NB - 1, None)
            both(NB - 1, None, None)


_INS = ['x', 'src', 'dst'] + ['L0_gnn_' + n for n in ('Wq', 'Wk', 'Wv', 'O_w', 'O_b', 'ln1_w', 'ln1_b', 'f1_w', 'f1_b', 'f2_w', 'f2_b',
        'ln2_w', 'ln2_b', 'gru_w_ih', 'gru_w_hh', 'gru_b_ih', 'gru_b_hh')] + ['L0_ffn_' + n for n in ('Wg', 'bg', 'bias', 'W1', 'b1', 'W2', 'b2')]


def kernel(**inputs):
    import numpy as _np
    import concourse.bacc as _bacc
    from concourse import mybir as _mybir
    from concourse.bass_utils import run_bass_kernel_spmd as _run

    nc = _bacc.Bacc("TRN2", target_bir_lowering=False, num_devices=1)
    arrays, args = {}, []
    for name in _INS:
        a = _np.ascontiguousarray(inputs[name])
        arrays[f"in_{name}_dram"] = a
        args.append(nc.dram_tensor(f"in_{name}_dram", a.shape, _mybir.dt.from_np(a.dtype), kind="ExternalInput").ap())
    args.append(nc.dram_tensor("out_0_dram", inputs["x"].shape, _mybir.dt.float32, kind="ExternalOutput").ap())
    gnn_moe_layer(nc, *args)
    r = _run(nc, [arrays], core_ids=[0])
    return r.results[0]["out_0_dram"]
```
